# Optimizing a Trainium2 kernel written in Bass

```python
import numpy as np
import jax
import jax.numpy as jnp

def _softmax(x, axis=-1):
    return jax.nn.softmax(x, axis=axis)
def _gelu(x):
    return jax.nn.gelu(x, approximate=True)
def _silu(x):
    return jax.nn.silu(x)
def _sigmoid(x):
    return jax.nn.sigmoid(x)
def _layernorm(x, axis=-1, eps=1e-5):
    m = jnp.mean(x, axis=axis, keepdims=True)
    v = jnp.var(x, axis=axis, keepdims=True)
    return (x - m) / jnp.sqrt(v + eps)
def _scatter_add(tgt, idx, src, axis=0):
    return tgt.at[idx].add(src)
def _segment_sum(src, seg, n):
    return jax.ops.segment_sum(src, seg, n)

kernel_name = 'mk_conv_seq_d2_conv_nchw128_3eda08'

def setup_inputs(seed: int = 0):
    np.random.seed(seed)
    _w = jnp.asarray
    def _rec_inputs():
        import jax
        import jax.numpy as jnp
        _gk = jax.random.key(seed)
        x = -0.0002023 + 1 * jax.random.normal(jax.random.fold_in(_gk, 1), (16, 128, 56, 56), jnp.float32)
        return x
    x = _rec_inputs()
    def _L0_conv_setup():
        import jax, jax.numpy as jnp
        import numpy as np
        B, C, H, W = (16, 128, 56, 56)
        QK, HEADS, NWIN, TOPK, MLPR = (128, 4, 7, 4, 3)
        HD_Q, HD_V = (QK // HEADS, C // HEADS)
        WH, WW = (H // NWIN, W // NWIN)
        P2, W2 = (NWIN * NWIN, WH * WW)
        SCALE = QK ** (-0.5)

        def _dwconv(x, w, b):
            y = jax.lax.conv_general_dilated(x, w, (1, 1), 'SAME', feature_group_count=x.shape[1], dimension_numbers=('NCHW', 'OIHW', 'NCHW'))
            return y + b[None, :, None, None]

        def _ln(x, g, b):
            m = x.mean(-1, keepdims=True)
            v = ((x - m) ** 2).mean(-1, keepdims=True)
            return (x - m) * jax.lax.rsqrt(v + 1e-06) * g + b

        def _win(t):
            b, _, _, c = t.shape
            return t.reshape(b, NWIN, WH, NWIN, WW, c).transpose(0, 1, 3, 2, 4, 5).reshape(b, P2, WH, WW, c)

        def _unwin(t):
            b, c = (t.shape[0], t.shape[-1])
            return t.reshape(b, NWIN, NWIN, WH, WW, c).transpose(0, 1, 3, 2, 4, 5).reshape(b, H, W, c)
        key = jax.random.key(seed)
        ks = jax.random.split(key, 8)
        p = lambda k, sh: (0.02 * jax.random.normal(k, sh)).astype(jnp.float32)
        return {'x': jax.random.normal(ks[0], (B, C, H, W), dtype=jnp.float32), 'pos_w': p(ks[1], (C, 1, 3, 3)), 'pos_b': jnp.zeros((C,), jnp.float32), 'ln1_g': jnp.ones((C,), jnp.float32), 'ln1_b': jnp.zeros((C,), jnp.float32), 'qkv_w': p(ks[2], (C, 2 * QK + C)), 'qkv_b': jnp.zeros((2 * QK + C,), jnp.float32), 'lepe_w': p(ks[3], (C, 1, 5, 5)), 'lepe_b': jnp.zeros((C,), jnp.float32), 'wo_w': p(ks[4], (C, C)), 'wo_b': jnp.zeros((C,), jnp.float32), 'ln2_g': jnp.ones((C,), jnp.float32), 'ln2_b': jnp.zeros((C,), jnp.float32), 'mlp_w1': p(ks[5], (C, MLPR * C)), 'mlp_b1': jnp.zeros((MLPR * C,), jnp.float32), 'mlp_w2': p(ks[6], (MLPR * C, C)), 'mlp_b2': jnp.zeros((C,), jnp.float32)}
    _L0_conv_all = _L0_conv_setup()
    _L0_conv_in = {k: v for k, v in _L0_conv_all.items() if k in ('pos_w', 'pos_b', 'ln1_g', 'ln1_b', 'qkv_w', 'qkv_b', 'lepe_w', 'lepe_b', 'wo_w', 'wo_b', 'ln2_g', 'ln2_b', 'mlp_w1', 'mlp_b1', 'mlp_w2', 'mlp_b2', )}
    del _L0_conv_all

    def _L1_conv_setup():
        import jax, jax.numpy as jnp
        import numpy as np
        G = 8
        K = 3
        KK = K * K
        PAD = 1

        def _conv1x1(x, w):
            return jnp.einsum('bchw,oc->bohw', x, w)

        def _deform_conv(feat, offset_feat, w_offmask, b_offmask, w_dcn, b_dcn):
            B, C, H, W = feat.shape
            Cg = C // G
            dt = feat.dtype
            om = jax.lax.conv_general_dilated(offset_feat, w_offmask, (1, 1), [(PAD, PAD), (PAD, PAD)], dimension_numbers=('NCHW', 'OIHW', 'NCHW')) + b_offmask[None, :, None, None]
            o1, o2, m = jnp.split(om, 3, axis=1)
            off = jnp.concatenate([o1, o2], axis=1).reshape(B, G, KK, 2, H, W)
            dy, dx = (off[:, :, :, 0], off[:, :, :, 1])
            mask = jax.nn.sigmoid(m).reshape(B, G, KK, H, W)
            ky = (jnp.arange(KK) // K - PAD).astype(dt)
            kx = (jnp.arange(KK) % K - PAD).astype(dt)
            yg = jnp.arange(H, dtype=dt)
            xg = jnp.arange(W, dtype=dt)
            py = yg[None, None, None, :, None] + ky[None, None, :, None, None] + dy
            px = xg[None, None, None, None, :] + kx[None, None, :, None, None] + dx
            y0 = jnp.floor(py)
            x0 = jnp.floor(px)
            ly = py - y0
            lx = px - x0
            y0i = y0.astype(jnp.int32)
            x0i = x0.astype(jnp.int32)
            src = feat.reshape(B, G, Cg, H * W)

            def corner(yi, xi, wgt):
                valid = (yi >= 0) & (yi < H) & (xi >= 0) & (xi < W)
                idx = jnp.clip(yi, 0, H - 1) * W + jnp.clip(xi, 0, W - 1)
                g = jnp.take_along_axis(src, idx.reshape(B, G, 1, KK * H * W), axis=3)
                wv = (wgt * valid).astype(dt)
                return g.reshape(B, G, Cg, KK, H, W) * wv[:, :, None]
            val = corner(y0i, x0i, (1 - ly) * (1 - lx)) + corner(y0i, x0i + 1, (1 - ly) * lx) + corner(y0i + 1, x0i, ly * (1 - lx)) + corner(y0i + 1, x0i + 1, ly * lx)
            val = val * mask[:, :, None]
            wr = w_dcn.reshape(w_dcn.shape[0], G, Cg, KK)
            return jnp.einsum('bgckhw,ogck->bohw', val, wr) + b_dcn[None, :, None, None]
        key = jax.random.key(seed)
        ks = jax.random.split(key, 9)
        B, C, H, W = (2, 128, 128, 128)
        return {'feat_l': jax.random.normal(ks[0], (B, C, H, W), jnp.float32), 'feat_s': jax.random.normal(ks[1], (B, C, H // 2, W // 2), jnp.float32), 'w_atten': jax.random.normal(ks[2], (C, C), jnp.float32) * 0.05, 'w_fsm': jax.random.normal(ks[3], (C, C), jnp.float32) * 0.05, 'w_off': jax.random.normal(ks[4], (C, 2 * C), jnp.float32) * 0.05, 'w_offmask': jax.random.normal(ks[5], (3 * G * KK, C, K, K), jnp.float32) * 0.02, 'b_offmask': jax.random.normal(ks[6], (3 * G * KK,), jnp.float32) * 0.01, 'w_dcn': jax.random.normal(ks[7], (C, C, K, K), jnp.float32) * 0.05, 'b_dcn': jax.random.normal(ks[8], (C,), jnp.float32) * 0.01}
    _L1_conv_all = _L1_conv_setup()
    _L1_conv_in = {k: v for k, v in _L1_conv_all.items() if k in ('feat_s', 'w_atten', 'w_fsm', 'w_off', 'w_offmask', 'b_offmask', 'w_dcn', 'b_dcn', )}
    del _L1_conv_all

    return {
        "x": x,
        "L0_conv_pos_w": _L0_conv_in["pos_w"],
        "L0_conv_pos_b": _L0_conv_in["pos_b"],
        "L0_conv_ln1_g": _L0_conv_in["ln1_g"],
        "L0_conv_ln1_b": _L0_conv_in["ln1_b"],
        "L0_conv_qkv_w": _L0_conv_in["qkv_w"],
        "L0_conv_qkv_b": _L0_conv_in["qkv_b"],
        "L0_conv_lepe_w": _L0_conv_in["lepe_w"],
        "L0_conv_lepe_b": _L0_conv_in["lepe_b"],
        "L0_conv_wo_w": _L0_conv_in["wo_w"],
        "L0_conv_wo_b": _L0_conv_in["wo_b"],
        "L0_conv_ln2_g": _L0_conv_in["ln2_g"],
        "L0_conv_ln2_b": _L0_conv_in["ln2_b"],
        "L0_conv_mlp_w1": _L0_conv_in["mlp_w1"],
        "L0_conv_mlp_b1": _L0_conv_in["mlp_b1"],
        "L0_conv_mlp_w2": _L0_conv_in["mlp_w2"],
        "L0_conv_mlp_b2": _L0_conv_in["mlp_b2"],
        "L1_conv_feat_s": _L1_conv_in["feat_s"],
        "L1_conv_w_atten": _L1_conv_in["w_atten"],
        "L1_conv_w_fsm": _L1_conv_in["w_fsm"],
        "L1_conv_w_off": _L1_conv_in["w_off"],
        "L1_conv_w_offmask": _L1_conv_in["w_offmask"],
        "L1_conv_b_offmask": _L1_conv_in["b_offmask"],
        "L1_conv_w_dcn": _L1_conv_in["w_dcn"],
        "L1_conv_b_dcn": _L1_conv_in["b_dcn"],
    }

def reference(x, L0_conv_pos_w, L0_conv_pos_b, L0_conv_ln1_g, L0_conv_ln1_b, L0_conv_qkv_w, L0_conv_qkv_b, L0_conv_lepe_w, L0_conv_lepe_b, L0_conv_wo_w, L0_conv_wo_b, L0_conv_ln2_g, L0_conv_ln2_b, L0_conv_mlp_w1, L0_conv_mlp_b1, L0_conv_mlp_w2, L0_conv_mlp_b2, L1_conv_feat_s, L1_conv_w_atten, L1_conv_w_fsm, L1_conv_w_off, L1_conv_w_offmask, L1_conv_b_offmask, L1_conv_w_dcn, L1_conv_b_dcn):
    import jax
    import jax.numpy as jnp
    def _L0_conv_ref(x, pos_w, pos_b, ln1_g, ln1_b, qkv_w, qkv_b, lepe_w, lepe_b, wo_w, wo_b, ln2_g, ln2_b, mlp_w1, mlp_b1, mlp_w2, mlp_b2):
        import jax, jax.numpy as jnp
        import numpy as np
        B, C, H, W = (16, 128, 56, 56)
        QK, HEADS, NWIN, TOPK, MLPR = (128, 4, 7, 4, 3)
        HD_Q, HD_V = (QK // HEADS, C // HEADS)
        WH, WW = (H // NWIN, W // NWIN)
        P2, W2 = (NWIN * NWIN, WH * WW)
        SCALE = QK ** (-0.5)

        def _dwconv(x, w, b):
            y = jax.lax.conv_general_dilated(x, w, (1, 1), 'SAME', feature_group_count=x.shape[1], dimension_numbers=('NCHW', 'OIHW', 'NCHW'))
            return y + b[None, :, None, None]

        def _ln(x, g, b):
            m = x.mean(-1, keepdims=True)
            v = ((x - m) ** 2).mean(-1, keepdims=True)
            return (x - m) * jax.lax.rsqrt(v + 1e-06) * g + b

        def _win(t):
            b, _, _, c = t.shape
            return t.reshape(b, NWIN, WH, NWIN, WW, c).transpose(0, 1, 3, 2, 4, 5).reshape(b, P2, WH, WW, c)

        def _unwin(t):
            b, c = (t.shape[0], t.shape[-1])
            return t.reshape(b, NWIN, NWIN, WH, WW, c).transpose(0, 1, 3, 2, 4, 5).reshape(b, H, W, c)
        x = x + _dwconv(x, pos_w, pos_b)
        xh = x.transpose(0, 2, 3, 1)
        y = _ln(xh, ln1_g, ln1_b)
        qkv = y @ qkv_w + qkv_b
        q, kv = (qkv[..., :QK], qkv[..., QK:])
        qw, kvw = (_win(q), _win(kv))
        q_win = jax.lax.stop_gradient(qw.mean((2, 3)))
        k_win = jax.lax.stop_gradient(kvw[..., :QK].mean((2, 3)))
        logits = jnp.einsum('bpc,bqc->bpq', q_win * SCALE, k_win)
        _, idx = jax.lax.top_k(logits, TOPK)
        kv_pix = kvw.reshape(B, P2, W2, QK + C)
        kv_sel = jax.vmap(lambda t, i: t[i])(kv_pix, idx)
        k_sel = kv_sel[..., :QK].reshape(B, P2, TOPK * W2, HEADS, HD_Q)
        v_sel = kv_sel[..., QK:].reshape(B, P2, TOPK * W2, HEADS, HD_V)
        q_pix = qw.reshape(B, P2, W2, HEADS, HD_Q)
        att = jnp.einsum('bpqhd,bpkhd->bphqk', q_pix * SCALE, k_sel)
        att = jax.nn.softmax(att, axis=-1)
        o = jnp.einsum('bphqk,bpkhd->bpqhd', att, v_sel).reshape(B, P2, W2, C)
        o = _unwin(o)
        v_img = kv[..., QK:].transpose(0, 3, 1, 2)
        lepe = _dwconv(v_img, lepe_w, lepe_b).transpose(0, 2, 3, 1)
        o = (o + lepe) @ wo_w + wo_b
        xh = xh + o
        z = _ln(xh, ln2_g, ln2_b)
        z = jax.nn.gelu(z @ mlp_w1 + mlp_b1, approximate=False) @ mlp_w2 + mlp_b2
        xh = xh + z
        return xh.transpose(0, 3, 1, 2)

    def _L1_conv_ref(feat_l, feat_s, w_atten, w_fsm, w_off, w_offmask, b_offmask, w_dcn, b_dcn):
        import jax, jax.numpy as jnp
        import numpy as np
        G = 8
        K = 3
        KK = K * K
        PAD = 1

        def _conv1x1(x, w):
            return jnp.einsum('bchw,oc->bohw', x, w)

        def _deform_conv(feat, offset_feat, w_offmask, b_offmask, w_dcn, b_dcn):
            B, C, H, W = feat.shape
            Cg = C // G
            dt = feat.dtype
            om = jax.lax.conv_general_dilated(offset_feat, w_offmask, (1, 1), [(PAD, PAD), (PAD, PAD)], dimension_numbers=('NCHW', 'OIHW', 'NCHW')) + b_offmask[None, :, None, None]
            o1, o2, m = jnp.split(om, 3, axis=1)
            off = jnp.concatenate([o1, o2], axis=1).reshape(B, G, KK, 2, H, W)
            dy, dx = (off[:, :, :, 0], off[:, :, :, 1])
            mask = jax.nn.sigmoid(m).reshape(B, G, KK, H, W)
            ky = (jnp.arange(KK) // K - PAD).astype(dt)
            kx = (jnp.arange(KK) % K - PAD).astype(dt)
            yg = jnp.arange(H, dtype=dt)
            xg = jnp.arange(W, dtype=dt)
            py = yg[None, None, None, :, None] + ky[None, None, :, None, None] + dy
            px = xg[None, None, None, None, :] + kx[None, None, :, None, None] + dx
            y0 = jnp.floor(py)
            x0 = jnp.floor(px)
            ly = py - y0
            lx = px - x0
            y0i = y0.astype(jnp.int32)
            x0i = x0.astype(jnp.int32)
            src = feat.reshape(B, G, Cg, H * W)

            def corner(yi, xi, wgt):
                valid = (yi >= 0) & (yi < H) & (xi >= 0) & (xi < W)
                idx = jnp.clip(yi, 0, H - 1) * W + jnp.clip(xi, 0, W - 1)
                g = jnp.take_along_axis(src, idx.reshape(B, G, 1, KK * H * W), axis=3)
                wv = (wgt * valid).astype(dt)
                return g.reshape(B, G, Cg, KK, H, W) * wv[:, :, None]
            val = corner(y0i, x0i, (1 - ly) * (1 - lx)) + corner(y0i, x0i + 1, (1 - ly) * lx) + corner(y0i + 1, x0i, ly * (1 - lx)) + corner(y0i + 1, x0i + 1, ly * lx)
            val = val * mask[:, :, None]
            wr = w_dcn.reshape(w_dcn.shape[0], G, Cg, KK)
            return jnp.einsum('bgckhw,ogck->bohw', val, wr) + b_dcn[None, :, None, None]
        B, C, H, W = feat_l.shape
        feat_up = jax.image.resize(feat_s, (B, C, H, W), method='bilinear')
        pooled = jnp.mean(feat_l, axis=(2, 3), keepdims=True)
        atten = jax.nn.sigmoid(jax.nn.relu(_conv1x1(pooled, w_atten)))
        x = feat_l + feat_l * atten
        feat_arm = jax.nn.relu(_conv1x1(x, w_fsm))
        offset_feat = jax.nn.relu(_conv1x1(jnp.concatenate([feat_arm, feat_up * 2.0], axis=1), w_off))
        feat_align = jax.nn.relu(_deform_conv(feat_up, offset_feat, w_offmask, b_offmask, w_dcn, b_dcn))
        return feat_align + feat_l

    def _gn(v, G=32, eps=1e-5):
        B_, C_, H_, W_ = v.shape
        g = v.reshape(B_, G, C_ // G, H_, W_)
        m = jnp.mean(g, axis=(2, 3, 4), keepdims=True)
        s = jnp.var(g, axis=(2, 3, 4), keepdims=True)
        return ((g - m) / jnp.sqrt(s + eps)).reshape(v.shape)

    def _ln_c(v, eps=1e-6):
        m = jnp.mean(v, axis=1, keepdims=True)
        s = jnp.var(v, axis=1, keepdims=True)
        return (v - m) / jnp.sqrt(s + eps)

    def _ln_t(v, eps=1e-5):
        m = jnp.mean(v, axis=-1, keepdims=True)
        s = jnp.var(v, axis=-1, keepdims=True)
        return (v - m) / jnp.sqrt(s + eps)

    def _to_tokens(v):
        B_, C_, H_, W_ = v.shape
        return v.reshape(B_, C_, H_ * W_).transpose(0, 2, 1)
    def _from_tokens(t, like):
        B_, C_, H_, W_ = like.shape
        return t.transpose(0, 2, 1).reshape(B_, C_, H_, W_)

    x = _L0_conv_ref(x, L0_conv_pos_w, L0_conv_pos_b, L0_conv_ln1_g, L0_conv_ln1_b, L0_conv_qkv_w, L0_conv_qkv_b, L0_conv_lepe_w, L0_conv_lepe_b, L0_conv_wo_w, L0_conv_wo_b, L0_conv_ln2_g, L0_conv_ln2_b, L0_conv_mlp_w1, L0_conv_mlp_b1, L0_conv_mlp_w2, L0_conv_mlp_b2)
    x = _L1_conv_ref(x, L1_conv_feat_s, L1_conv_w_atten, L1_conv_w_fsm, L1_conv_w_off, L1_conv_w_offmask, L1_conv_b_offmask, L1_conv_w_dcn, L1_conv_b_dcn)
    return x


_drawn_inputs = setup_inputs


def setup_inputs(seed=0):
    import zlib

    import numpy as np

    out = dict(_drawn_inputs(seed))
    spreads = {'L0_conv_pos_b': (0.0, 0.1),
     'L0_conv_ln1_g': (1.0, 0.6),
     'L0_conv_ln1_b': (0.0, 0.8),
     'L0_conv_qkv_b': (0.0, 0.325),
     'L0_conv_lepe_b': (0.0, 0.331),
     'L0_conv_wo_b': (0.0, 0.1),
     'L0_conv_ln2_g': (1.0, 0.6),
     'L0_conv_ln2_b': (0.0, 0.8),
     'L0_conv_mlp_b1': (0.0, 0.407),
     'L0_conv_mlp_b2': (0.0, 0.1)}
    factors = {'L0_conv_qkv_w': 6.765,
     'L0_conv_lepe_w': 8.0,
     'L1_conv_w_atten': 8.0,
     'L1_conv_b_offmask': 8.0,
     'L1_conv_b_dcn': 8.0}
    for name, (base, spread) in spreads.items():
        noise = np.random.default_rng([zlib.crc32(name.encode()), seed]).standard_normal(out[name].shape)
        drawn = base * np.exp(spread * noise) if base else spread * noise
        out[name] = jnp.asarray(drawn.astype(out[name].dtype))
    for name, factor in factors.items():
        out[name] = (out[name] * factor).astype(out[name].dtype)
    return out
```

```python
from contextlib import ExitStack

import numpy as np

import concourse.bass as bass
from concourse import mybir

F32 = mybir.dt.float32
U32 = mybir.dt.uint32
ALU = mybir.AluOpType
ACT = mybir.ActivationFunctionType
AX = mybir.AxisListType

B, C, H, W = 16, 128, 56, 56
NIMG = B
PIX = H * W
HEADS, HD, NWIN, WS, TOPK = 4, 32, 7, 8, 4
P2, W2 = NWIN * NWIN, WS * WS
BAND = WS * W
NB = NWIN
HID = 3
SCALE = float(C) ** -0.5
SH, SW = 64, 64
G, KK, CG = 8, 9, 16
S = G * KK
TS_ = W + 2
NBLK = -(-TS_ * TS_ // 128)
TROWS = NBLK * 128 * G
FPAD = NBLK * 128 + TS_ + 1
PATCH = 4 * CG
SP57 = W + 1
NT = 25
POS = NT * 128
OFLEN = 1 + SP57 + POS + SP57 + 1
MAGIC = 12582912.0
NSLOT = 3
NH = 32
NS = S - NH
WR = 8
WUP = 2
XP = 64
FROW = 1 + WUP
NROWS = (NT * 128 - 1 - 8) // SP57 + WR + 2
_ALL = [(g, k) for g in range(G) for k in range(KK)]
ORDER = _ALL[NH:] + _ALL[:NH]
GH = _ALL[NH - 1][0] + 1
SLOT_USES = [len(range(s, NT, NSLOT)) for s in range(NSLOT)]
NKV = 3
KV_USES = [len(range(s, P2, NKV)) for s in range(NKV)]
NTB = 4
TB_USES = [len(range(s, NBLK, NTB)) for s in range(NTB)]

CONSTS = {}


def const_layout():
    at = 0
    for name, n in (("ident", 128), ("fold", 64), ("mean", 128), ("posy", NT), ("posx", NT), ("kyx", 2 * S),
                    ("gidx", S), ("ibase", B), ("rowk", NH * WR), ("iota", XP), ("wres", 4 * H), ("wbat", 2 * B), ("eps", 1)):
        CONSTS[name] = (at, n)
        at += n
    return at


NCONST = const_layout()


def resize_matrix(n_in, n_out):
    inv = np.float32(n_in / n_out)
    kscale = max(inv, np.float32(1.0))
    at = (np.arange(n_out, dtype=np.float32) + np.float32(0.5)) * inv - np.float32(0.5)
    x = np.abs(at[None, :] - np.arange(n_in, dtype=np.float32)[:, None]) / kscale
    w = np.maximum(np.float32(0), np.float32(1) - x)
    return (w / w.sum(0, keepdims=True)).astype(np.float32)


def constants():
    c = np.zeros((128, NCONST), np.float32)

    def put(name, v):
        a, n = CONSTS[name]
        c[:, a:a + n] = v

    put("ident", np.eye(128))
    put("fold", np.concatenate([np.eye(64), np.eye(64)], 0))
    put("mean", 1.0 / C)
    pos = np.arange(NT)[None, :] * 128 + np.arange(128)[:, None]
    put("posy", pos // SP57)
    put("posx", pos % SP57)
    k = np.array([k for _, k in ORDER])
    put("kyx", np.concatenate([k // 3 - 1, k % 3 - 1])[None])
    put("gidx", (np.array([g for g, _ in ORDER]) + (TS_ + 1) * G)[None])
    put("rowk", (k[NS:, None] // 3 - 1 - WUP + np.arange(WR)).reshape(1, -1))
    put("iota", np.arange(XP)[None])
    put("ibase", (np.arange(B) * TROWS)[None])
    m = resize_matrix(SH, H)
    wres = np.zeros((4, H), np.float32)
    for y in range(H):
        for t in range(4):
            src = 8 * (y // 7) + y % 7 + t - 1
            if 0 <= src < SH:
                wres[t, y] = m[src, y]
    put("wres", wres.reshape(1, -1))
    mb = resize_matrix(2, B)
    put("wbat", mb.T.reshape(1, -1))
    put("eps", 1e-6)
    return c


def build(nc, a, out):
    table = nc.dram_tensor("patch_table", (NIMG * TROWS, PATCH), F32, kind="Internal").ap()
    fup = nc.dram_tensor("feat_up_twice", (NIMG, C, PIX), F32, kind="Internal").ap()
    qd = nc.dram_tensor("q_windows", (P2, C, W2), F32, kind="Internal").ap()
    kd = nc.dram_tensor("k_windows", (P2, C, W2), F32, kind="Internal").ap()
    vd = nc.dram_tensor("v_windows", (P2, W2, C), F32, kind="Internal").ap()

    with ExitStack() as ctx:
        def sb(name, shape, dt=F32, c=ctx):
            return c.enter_context(nc.sbuf_tensor(name, shape, dt))

        def sem(name):
            return ctx.enter_context(nc.semaphore(name))

        bank = [ctx.enter_context(nc.psum_tensor(f"bank{n}", [128, 512], F32)) for n in range(8)]
        cst = sb("cst", [128, NCONST])

        def const(name):
            at, n = CONSTS[name]
            return cst[:, at:at + n]

        tctx = ExitStack()
        src_s = [sb(f"src{s}", [128, (SH + 2) * SW], c=tctx) for s in range(2)]
        rows_s = sb("rows_s", [128, H, SW + 2], c=tctx)
        prod_s = sb("prod_s", [128, H * SW], c=tctx)
        up_s = [sb(f"up{s}", [128, H, W], c=tctx) for s in range(2)]
        fpad = sb("fpad", [128, FPAD], c=tctx)
        fdense = sb("fdense", [128, PIX], c=tctx)
        bcol = sb("bcol", [128, 2], c=tctx)
        tst = [sb(f"tst{s}", [128, G, 4, CG], c=tctx) for s in range(NTB)]
        tctx.close()

        wqkv = sb("wqkv", [128, 3 * C])
        wo = sb("wo", [128, C])
        w1 = sb("w1", [128, HID * C])
        w2 = sb("w2", [128, HID, C])
        wfsm = sb("wfsm", [128, C])
        watt = sb("watt", [128, C])
        woff = sb("woff", [128, 2, C])
        wom = sb("wom", [128, KK, 3 * S])
        wdcn = sb("wdcn", [128, KK, C])
        posw = sb("posw", [128, 9])
        lepw = sb("lepw", [128, 25])
        cols = sb("cols", [128, 16])
        POSB, G1, B1, BQ, BK, BV, LB, BO, G2, B2, M2, BD, M1, BQS = 0, 1, 2, 3, 4, 5, 6, 7, 8, 9, 10, 11, 12, 15
        bvrow = sb("bvrow", [64, C])
        bom = sb("bom", [128, 3 * S])
        kyxb = sb("kyxb", [128, 2 * S])
        gimg = sb("gimg", [128, S])

        def col(n):
            return cols[:, n:n + 1]

        xpad = sb("xpad", [128, H + 4, W + 4])
        xw = sb("xw", [128, PIX])
        t1 = sb("t1", [128, BAND])
        t2 = sb("t2", [128, BAND])
        yw = sb("yw", [128, BAND])
        qb = [sb(f"qb{s}", [128, BAND]) for s in range(2)]
        kb = [sb(f"kb{s}", [128, BAND]) for s in range(2)]
        vb = sb("vb", [64, NWIN, C])
        qm = sb("qm", [128, P2])
        km = sb("km", [128, P2])
        lg = sb("lg", [64, P2])
        mx8 = sb("mx8", [64, 8])
        ix8 = sb("ix8", [64, 8], U32)
        sel = sb("sel", [1, P2 * TOPK], U32)
        qbd = sb("qbd", [128, NWIN, HEADS, W2])
        ksel = [sb(f"ksel{s}", [128, TOPK * W2]) for s in range(NKV)]
        vsel = [sb(f"vsel{s}", [128, 2, C]) for s in range(NKV)]
        nmx = [sb(f"nmx{s}", [128, 2]) for s in range(2)]
        sm = [sb(f"sm{s}", [128, 2]) for s in range(2)]
        rinv = sb("rinv", [128, 2])
        pr = [sb(f"pr{s}", [128, 2, TOPK * W2]) for s in range(2)]
        pt = [sb(f"pt{s}", [128, 2, 2, 128]) for s in range(2)]
        osb = [sb(f"osb{s}", [128, C]) for s in range(2)]
        ol = sb("ol", [128, BAND])
        hid = sb("hid", [128, HID, BAND])
        pool1 = sb("pool1", [128, 4])

        xd = sb("xd", [128, POS])
        ofp = sb("ofp", [128, OFLEN])
        gbuf = [sb(f"gbuf{s}", [128, NS, 2, 2, CG]) for s in range(NSLOT)]
        wts = [sb(f"wts{s}", [128, S, 2, 2]) for s in range(NSLOT)]
        idx = [sb(f"idx{s}", [128, S], U32) for s in range(NSLOT)]
        pyx = sb("pyx", [128, 2 * S])
        fl = sb("fl", [128, 2 * S])
        tmp = sb("tmp", [128, 2 * S])
        msk = sb("msk", [128, S])
        ady = sb("ady", [128, S, 2])
        val = sb("val", [128, NS * CG])
        hxt = sb("hxt", [128, NH, XP])
        hxs = sb("hxs", [128, NH // 2, 128])
        fx = sb("fx", [128, GH, NROWS, CG])
        pyr = sb("pyr", [128, NH])
        wy = sb("wy", [128, NH, WR])
        prod = sb("prod", [128, 4, WR, CG])
        vh = [sb(f"vh{s}", [128, NH * CG]) for s in range(NSLOT)]
        vio = sb("vio", [128, NH])
        vmx = sb("vmx", [128, 2])
        flag = sb("flag", [1, NT], U32)
        valt = hid[:].rearrange("p m n -> p (m n)")[:, 0:KK * 128].rearrange("p (k n) -> p k n", k=KK)
        rt = sb("rt", [128, 128])

        s_w = sem("weights_loaded")
        s_src = sem("small_maps_loaded")
        s_z = sem("table_borders_zeroed")
        s_up = sem("table_image_ready")
        s_tmm = sem("table_block_turned")
        s_tev = [sem(f"table_block_copied{s}") for s in range(NTB)]
        s_tst = [sem(f"table_block_stored{s}") for s in range(NTB)]
        s_fst = sem("feat_up_stored")
        s_mz = sem("main_borders_zeroed")
        s_setup = sem("bias_constants_ready")
        s_xin = sem("x_loaded")
        s_xc = sem("x_padded")
        s_xpos = sem("pos_conv_done")
        s_mm = sem("qkv_phase_matmul")
        s_d = sem("centred")
        s_sq = sem("squared")
        s_sd = sem("deviation_ready")
        s_y = sem("normed_ready")
        s_q = sem("q_band_ready")
        s_k = sem("k_band_ready")
        s_vc = sem("v_padded")
        s_v = sem("v_band_ready")
        s_qst = [sem(f"q_band_stored{s}") for s in range(2)]
        s_kst = [sem(f"k_band_stored{s}") for s in range(2)]
        s_vst = sem("v_band_stored")
        s_qm = sem("window_means_ready")
        s_lg = sem("logits_ready")
        s_ix = sem("topk_ready")
        s_sel = sem("topk_flat")
        s_qbd = sem("queries_loaded")
        s_kv = [sem(f"kv_selected{s}") for s in range(NKV)]
        s_sc = sem("scores_ready")
        s_mx = sem("max_ready")
        s_ex = sem("probs_ready")
        s_tr = sem("probs_turned")
        s_pt = sem("probs_turned_copied")
        s_pv = sem("pv_ready")
        s_os = sem("heads_scaled")
        s_ot = sem("attention_band_turned")
        s_ol = sem("attention_plus_lepe")
        s_post = sem("post_phase_matmul")
        s_xa = sem("attention_residual")
        s_d2 = sem("centred2")
        s_sq2 = sem("squared2")
        s_sd2 = sem("deviation2_ready")
        s_z2 = sem("normed2_ready")
        s_gl = sem("gelu_ready")
        s_xm = sem("mlp_residual")
        s_pl = sem("pooled")
        s_gm = sem("gate_matmul")
        s_ge = sem("gate_exp")
        s_fi = sem("gated_band")
        s_p5 = sem("offset_feature_matmul")
        s_fa = sem("feat_arm_ready")
        s_ub = sem("feat_up_band_loaded")
        s_of = sem("offset_features_ready")
        s_xd = sem("x_handed_over")
        s_om = sem("offsets_matmul")
        s_mb = sem("mask_logits_ready")
        s_me = sem("mask_exp_ready")
        s_ir = sem("indices_ready")
        s_g = [sem(f"gathered{s}") for s in range(NSLOT)]
        s_gs = sem("gather_started")
        s_val = sem("samples_ready")
        s_vt = sem("samples_turned")
        s_ve = sem("samples_turned_copied")
        s_do = sem("deform_matmul")
        s_hx = sem("column_distance_ready")
        s_h2 = sem("column_hats_ready")
        s_wy = sem("row_distance_ready")
        s_wy2 = sem("row_hats_ready")
        s_ht = sem("column_hats_turned")
        s_hc = sem("column_hats_copied")
        s_hm = sem("window_matmul")
        s_hp = sem("window_weighted")
        s_vm = sem("outside_window_found")
        s_fm = sem("outside_window_matmul")
        s_fl = sem("general_path_flag")
        s_fb = sem("general_path_gathered")
        s_fbd = sem("general_path_over")
        s_vh = sem("hat_samples_ready")
        s_fx = sem("map_columns_loaded")
        s_fx2 = sem("map_columns_doubled")
        s_rt = sem("deform_relu")
        s_fin = sem("tile_finished")
        s_out = sem("image_stored")
        s_hold = {e: sem(f"hold_{e}") for e in ("sp", "pool", "pe", "dve")}

        block = ctx.enter_context(nc.Block())

        def hold(eng, name):
            eng.sem_inc(s_hold[name], 1)

        def band(t, b):
            return t[:, b * BAND:(b + 1) * BAND]

        def img(b):
            return lambda t: t.rearrange("p (r w c) -> p r w c", r=WS, c=WS)

        def win(t):
            return t.rearrange("p (w r c) -> p r w c", w=NWIN, c=WS)

        def rows57(t, off, b):
            at = off + b * WS * SP57
            return t[:, at:at + WS * SP57].rearrange("p (r c) -> p r c", c=SP57)[:, :, 0:W]

        def whole(body):
            body(0, None, False)
            body(1, 0, False)

        @block.sync
        def _(sp):
            loads = [
                (cst[:], a["consts"]), (wqkv[:], a["qkv_w"]), (wo[:], a["wo_w"]), (w1[:], a["mlp_w1"]),
                (w2[:], a["mlp_w2"].rearrange("(k p) o -> p k o", p=128)),
                (wfsm[:], a["w_fsm_t"]), (watt[:], a["w_atten_t"]),
                (woff[:], a["w_off_t"].rearrange("(k p) o -> p k o", p=128)),
                (wom[:], a["w_om_t"]), (wdcn[:], a["w_dcn_t"]),
                (posw[:], a["pos_w"]), (lepw[:], a["lepe_w"]), (cols[:, 0:15], a["cols"]),
                (bvrow[:], a["bv"].partition_broadcast(64)), (bom[:], a["b_om"].partition_broadcast(128)),
            ]
            sp.wait_ge(s_z, 1)
            for s in range(2):
                sp.dma_start(src_s[s][:, SW:SW + SH * SW], a["feat_s"][s]).then_inc(s_src, 16)
            sp.dma_start(cst[:], a["consts"]).then_inc(s_src, 16)

            def table_stores(i, first):
                sp.wait_ge(s_up, i + 1)
                sp.dma_start(fup[bass.ds(i, 1)].rearrange("a p n -> p (a n)"), fdense[:]).then_inc(s_fst, 16)
                for r in range(NBLK):
                    s = r % NTB
                    sp.wait_ge(s_tev[s], i * TB_USES[s] + r // NTB + 1)
                    dst = table[bass.ds(i * TROWS + r * 128 * G, 128 * G)]
                    sp.dma_start(dst.rearrange("(p g) e -> p (g e)", g=G),
                                 tst[s][:].rearrange("p g q c -> p (g q c)")).then_inc(s_tst[s], 16)

            table_stores(0, True)
            with sp.Fori(1, NIMG) as i:
                table_stores(i, False)
            sp.wait_ge(s_fst, 16 * NIMG)
            for s in range(NTB):
                sp.wait_ge(s_tst[s], 16 * NIMG * TB_USES[s])
            for dst, src in loads[1:]:
                sp.dma_start(dst, src).then_inc(s_w, 16)

            def x_qkv(i):
                if not (isinstance(i, int) and i == 0):
                    sp.wait_ge(s_xd, i)
                sp.dma_start(xw[:], a["x"][bass.ds(i, 1)].rearrange("a p n -> p (a n)")).then_inc(s_xin, 16)
                for b in range(NB):
                    w0 = b * NWIN
                    sp.wait_ge(s_q, i * NB + b + 1)
                    sp.dma_start(qd[w0:w0 + NWIN].rearrange("w p n -> p w n"),
                                 qb[b % 2][:].rearrange("p (w n) -> p w n", w=NWIN)).then_inc(s_qst[b % 2], 16)
                    sp.wait_ge(s_k, i * NB + b + 1)
                    sp.dma_start(kd[w0:w0 + NWIN].rearrange("w p n -> p w n"),
                                 kb[b % 2][:].rearrange("p (w n) -> p w n", w=NWIN)).then_inc(s_kst[b % 2], 16)
                    sp.wait_ge(s_v, i * NB + b + 1)
                    sp.dma_start(vd[w0:w0 + NWIN].rearrange("w n c -> n w c"), vb[:]).then_inc(s_vst, 16)

            def x_select(i):
                sp.wait_ge(s_ix, i + 1)
                sp.dma_start(sel[:], ix8[0:P2, 0:TOPK]).then_inc(s_sel, 16)
                for s in range(2):
                    n = (NB + 1 - s) // 2
                    sp.wait_ge(s_qst[s], i * (16 * n) + 16 * n)
                    sp.wait_ge(s_kst[s], i * (16 * n) + 16 * n)
                sp.wait_ge(s_vst, i * (16 * NB) + 16 * NB)
                sp.wait_ge(s_sel, i * 16 + 16)
                hold(sp, "sp")

            def x_band(i, b):
                if b > 0:
                    sp.wait_ge(s_sc, i * P2 + b * NWIN)
                for h in range(HEADS):
                    sp.dma_start(qbd[h * HD:(h + 1) * HD, :, h, :],
                                 qd[b * NWIN:(b + 1) * NWIN, h * HD:(h + 1) * HD].rearrange("w p n -> p w n")
                                 ).then_inc(s_qbd, 16)
                for j in range(NWIN):
                    n = b * NWIN + j
                    s = n % NKV
                    if n >= NKV:
                        sp.wait_ge(s_pv, i * P2 + n - NKV + 1)
                        hold(sp, "sp")
                    for m in range(TOPK):
                        w = sp.value_load(sel[0:1, n * TOPK + m:n * TOPK + m + 1], min_val=0, max_val=P2 - 1)
                        sp.dma_start(ksel[s][:, m * W2:(m + 1) * W2],
                                     kd[bass.ds(w, 1)].rearrange("a p n -> p (a n)")).then_inc(s_kv[s], 16)
                        sp.dma_start(vsel[s][(m % 2) * 64:(m % 2) * 64 + 64, m // 2, :],
                                     vd[bass.ds(w, 1)].rearrange("a n c -> n (a c)")).then_inc(s_kv[s], 16)

            def x_offsets(i):
                for b in range(NB):
                    sp.wait_ge(s_p5, i * 2 * NB + 2 * b) if b else sp.wait_ge(s_xm, i * NB + NB)
                    sp.dma_start(hid[:, 1, :], fup[bass.ds(i, 1), :, b * BAND:(b + 1) * BAND].rearrange(
                        "a p n -> p (a n)")).then_inc(s_ub, 16)

            def map_columns(i):
                if not (isinstance(i, int) and i == 0):
                    sp.wait_ge(s_hp, i * (8 * NT))
                t3 = table[bass.ds(i * TROWS, TROWS)].rearrange("(p g) e -> p g e", g=G)
                at = TS_ + 1
                for g in range(GH):
                    src = t3[at:at + H * TS_, g, 0:CG].rearrange("(y x) c -> x y c", x=TS_)[0:W]
                    sp.dma_start(fx[0:W, g, FROW:FROW + H, :], src).then_inc(s_fx, 16)
                sp.wait_ge(s_fx, i * (16 * GH) + 16 * GH)
                sp.dma_start(fx[XP:XP + W].rearrange("p g r c -> p (g r c)"),
                             fx[0:W].rearrange("p g r c -> p (g r c)")).then_inc(s_fx2, 16)

            def store(i):
                sp.wait_ge(s_fin, i * NT + NT)
                sp.dma_start(out[bass.ds(i, 1)].rearrange("a p h w -> p (a h) w"),
                             xd[:, 0:H * SP57].rearrange("p (h w) -> p h w", w=SP57)[:, :, 0:W]
                             ).then_inc(s_out, 16)

            def body(xi, di, tail):
                if tail:
                    store(di - 1)
                if xi is not None:
                    x_qkv(xi)
                    x_select(xi)
                    for b in range(NB):
                        x_band(xi, b)
                    x_offsets(xi)
                    map_columns(xi)

            sp.wait_ge(s_mz, 1)
            body(0, None, False)
            body(1, 0, False)
            with sp.Fori(2, NIMG) as i:
                body(i, i - 1, True)
            body(None, NIMG - 1, True)
            store(NIMG - 1)
            sp.wait_ge(s_out, 16 * NIMG)

        @block.gpsimd
        def _(pool):
            def gathers(i, first):
                for t in range(NT):
                    s = t % NSLOT
                    pool.wait_ge(s_ir, i * NT + t + 1)
                    hold(pool, "pool")
                    if not (first and t < NSLOT):
                        pool.inc_swdge_sem([s_g[s]], [16 * NS], mode="sub")
                    pool.sem_inc(s_gs, 1)
                    for k in range(NS):
                        pool.indirect_dma_start(gbuf[s][:, k].rearrange("p y x c -> p (y x c)"), None, table,
                                                bass.IndirectOffsetOnAxis(ap=idx[s][:, k:k + 1], axis=0)
                                                ).then_inc(s_g[s], 16)
                    if t >= 2:
                        general(i, t - 2)
                general(i, NT - 2)
                general(i, NT - 1)

            def general(i, t):
                pool.wait_ge(s_fl, i * NT + t + 1)
                hold(pool, "pool")
                f = pool.value_load(flag[0:1, t:t + 1], min_val=0, max_val=1)
                with pool.If(f > 0):
                    pool.wait_ge(s_hp, i * (8 * NT) + 8 * min(t + 3, NT))
                    hold(pool, "pool")
                    if not (isinstance(i, int) and i == 0 and t == 0):
                        pool.wait_ge(s_vh, i * NT + t)
                        hold(pool, "pool")
                    for h in range(NH):
                        pool.indirect_dma_start(hxt[:, h, :], None, table,
                                                bass.IndirectOffsetOnAxis(ap=idx[t % NSLOT][:, NS + h:NS + h + 1], axis=0)
                                                ).then_inc(s_fb, 16)
                    pool.wait_ge(s_fb, 16 * NH)
                    hold(pool, "pool")
                    pool.inc_swdge_sem([s_fb], [16 * NH], mode="sub")
                pool.sem_inc(s_fbd, 1)

            gathers(0, True)
            with pool.Fori(1, NIMG) as i:
                gathers(i, False)

        @block.tensor
        def _(pe):
            ident = const("ident")
            def table_turns(i, first):
                pe.wait_ge(s_up, i + 1)
                for r in range(NBLK):
                    s = r % NTB
                    if not (first and r < NTB):
                        pe.wait_ge(s_tev[s], i * TB_USES[s] + r // NTB)
                    for q in range(4):
                        dy, dx = q // 2, q % 2
                        mm = pe.matmul(bank[s][:, q * 128:(q + 1) * 128],
                                       fpad[:, r * 128 + dy * TS_ + dx:(r + 1) * 128 + dy * TS_ + dx], ident,
                                       start=True, stop=True, is_transpose=True)
                    mm.then_inc(s_tmm, 1)

            table_turns(0, True)
            with pe.Fori(1, NIMG) as i:
                table_turns(i, False)

            def x_qkv(i, bands):
                pe.wait_ge(s_xpos, i + 1)
                for b in bands:
                    n = i * NB + b + 1
                    if b > bands[0]:
                        pe.wait_ge(s_d, n - 1)
                    pe.matmul(bank[0][:, 0:BAND], const("mean"), band(xw, b), start=True, stop=True).then_inc(s_mm, 1)
                    pe.wait_ge(s_sq, n)
                    pe.matmul(bank[1][:, 0:BAND], const("mean"), t2[:], start=True, stop=True).then_inc(s_mm, 1)
                    pe.wait_ge(s_y, n)
                    for m in range(3):
                        pe.matmul(bank[2 + m][:, 0:BAND], wqkv[:, m * C:(m + 1) * C], yw[:],
                                  start=True, stop=True).then_inc(s_mm, 1)
                    for j in range(NWIN):
                        mm = pe.matmul(bank[5 + j // 4][0:64, (j % 4) * C:(j % 4 + 1) * C], yw[:, j * W2:(j + 1) * W2],
                                       wqkv[:, 2 * C:3 * C], start=True, stop=True)
                        if j in (3, NWIN - 1):
                            mm.then_inc(s_mm, 1)
                pe.wait_ge(s_qm, i * NB + bands[-1] + 1)
                pe.sem_inc(s_hold["pe"], 1)

            def x_route(i):
                pe.matmul(bank[7][0:P2, 0:P2], qm[:], km[:], start=True, stop=True).then_inc(s_lg, 1)

            def x_band(i, b):
                base = i * P2 + b * NWIN

                def scores(j):
                    n = b * NWIN + j
                    s = n % NKV
                    if j == 0:
                        pe.wait_ge(s_qbd, i * (64 * NB) + 64 * (b + 1))
                        pe.wait_ge(s_ix, i + 1)
                    pe.wait_ge(s_kv[s], i * (128 * KV_USES[s]) + 128 * (n // NKV + 1))
                    if j >= 2:
                        pe.wait_ge(s_ex, base + j - 1)
                    for h in range(2):
                        mm = pe.matmul(bank[2 + n % 2][:, h * 256:(h + 1) * 256],
                                       qbd[:, j, 2 * h:2 * h + 2, :].rearrange("p h q -> p (h q)"), ksel[s][:],
                                       start=True, stop=True)
                    mm.then_inc(s_sc, 1)

                def turn(j):
                    n = b * NWIN + j
                    pe.wait_ge(s_ex, base + j + 1)
                    for h in range(2):
                        for m in range(2):
                            mm = pe.transpose(bank[4 + n % 2][:, (2 * h + m) * 128:(2 * h + m + 1) * 128],
                                              pr[n % 2][:, h, m * 128:(m + 1) * 128], ident)
                    mm.then_inc(s_tr, 1)

                def pv(j):
                    n = b * NWIN + j
                    pe.wait_ge(s_pt, base + j + 1)
                    if j >= 1:
                        pe.wait_ge(s_os, base + j)
                    for h in range(2):
                        for m in range(2):
                            mm = pe.matmul(bank[6][:, h * C:(h + 1) * C], pt[n % 2][:, h, m, :],
                                           vsel[n % NKV][:, m, :], start=(m == 0), stop=(m == 1))
                    mm.then_inc(s_pv, 1)

                def turn_out(j):
                    n = b * NWIN + j
                    pe.wait_ge(s_os, base + j + 1)
                    mm = pe.matmul(bank[7][:, j * W2:(j + 1) * W2], osb[n % 2][:], const("fold"),
                                   start=True, stop=True)
                    if j == NWIN - 1:
                        mm.then_inc(s_ot, 1)

                for t in range(NWIN + 3):
                    if t < NWIN:
                        scores(t)
                    if 0 <= t - 1 < NWIN:
                        turn(t - 1)
                    if 0 <= t - 2 < NWIN:
                        pv(t - 2)
                    if 0 <= t - 3 < NWIN:
                        turn_out(t - 3)
                n = i * NB + b + 1
                pe.wait_ge(s_ol, n)
                pe.matmul(bank[0][:, 0:BAND], wo[:], ol[:], start=True, stop=True).then_inc(s_post, 1)
                pe.wait_ge(s_xa, n)
                pe.matmul(bank[1][:, 0:BAND], const("mean"), band(xw, b), start=True, stop=True).then_inc(s_post, 1)
                pe.wait_ge(s_sq2, n)
                pe.matmul(bank[0][:, 0:BAND], const("mean"), t2[:], start=True, stop=True).then_inc(s_post, 1)
                pe.wait_ge(s_z2, n)
                for m in range(HID):
                    pe.matmul(bank[2 + m][:, 0:BAND], w1[:, m * C:(m + 1) * C], yw[:],
                              start=True, stop=True).then_inc(s_post, 1)
                for m in range(HID):
                    pe.wait_ge(s_gl, i * (HID * NB) + HID * b + m + 1)
                    mm = pe.matmul(bank[5][:, 0:BAND], w2[:, m, :], hid[:, m, :], start=(m == 0), stop=(m == HID - 1))
                mm.then_inc(s_post, 1)
                pe.wait_ge(s_xm, n)
                pe.sem_inc(s_hold["pe"], 1)

            def x_offsets(i):
                pe.wait_ge(s_pl, i + 1)
                pe.matmul(bank[0][:, 0:1], watt[:], pool1[:, 0:1], start=True, stop=True).then_inc(s_gm, 1)
                for b in range(NB):
                    n = i * NB + b + 1
                    pe.wait_ge(s_fi, n)
                    pe.matmul(bank[0][:, 0:BAND], wfsm[:], t1[:], start=True, stop=True).then_inc(s_p5, 1)
                    pe.wait_ge(s_fa, n)
                    pe.wait_ge(s_ub, i * (16 * NB) + 16 * (b + 1))
                    for m in range(2):
                        mm = pe.matmul(bank[1][:, 0:BAND], woff[:, m, :], hid[:, m, :], start=(m == 0), stop=(m == 1))
                    mm.then_inc(s_p5, 1)
                pe.wait_ge(s_of, i * NB + NB)
                pe.sem_inc(s_hold["pe"], 1)

            def offsets(i, t):
                pe.wait_ge(s_of, i * NB + NB)
                if t:
                    pe.wait_ge(s_fl, i * NT + t)
                for k in range(KK):
                    at = 1 + SP57 + t * 128 + (k // 3 - 1) * SP57 + k % 3 - 1
                    mm = pe.matmul(bank[0][:, 0:3 * S], ofp[:, at:at + 128], wom[:, k, :],
                                   start=(k == 0), stop=(k == KK - 1))
                mm.then_inc(s_om, 1)

            def windows(i, t):
                pe.wait_ge(s_h2, i * NT + t + 1)
                for q in range(4):
                    if q >= 2:
                        pe.wait_ge(s_hc, i * (4 * NT) + 4 * t + q - 1)
                    for j in range(4):
                        p = 4 * q + j
                        mm = pe.transpose(bank[5 + q % 2][:, j * 128:(j + 1) * 128],
                                          hxt[:, 2 * p:2 * p + 2, :].rearrange("p a x -> p (a x)"), ident)
                    mm.then_inc(s_ht, 1)
                pe.wait_ge(s_vm, i * NT + t + 1)
                pe.matmul(bank[0][0:1, 0:1], vmx[:, 1:2], const("mean")[:, 0:1], start=True, stop=True).then_inc(s_fm, 1)
                pe.wait_ge(s_fx, i * (16 * GH) + 16 * GH)
                pe.wait_ge(s_fx2, i * 16 + 16)
                pe.sem_inc(s_hold["pe"], 1)
                y0 = t * 128 // SP57
                for q in range(4):
                    pe.wait_ge(s_hc, i * (4 * NT) + 4 * t + q + 1)
                    if q >= 2:
                        pe.wait_ge(s_hp, i * (8 * NT) + 8 * t + 2 * q - 2)
                    last = [None, None]
                    for j in range(4):
                        for a in range(2):
                            h = 8 * q + 2 * j + a
                            g, k = ORDER[NS + h]
                            row = y0 + k // 3 - 1 - WUP + FROW
                            last[a] = pe.matmul(bank[1 + 2 * (q % 2) + a][:, j * 128:(j + 1) * 128],
                                                hxs[XP * a:XP * a + XP, 4 * q + j, :],
                                                fx[XP * a:XP * a + XP, g, row:row + WR, :].rearrange("p r c -> p (r c)"),
                                                start=True, stop=True)
                    for a in range(2):
                        last[a].then_inc(s_hm, 1)

            def back(i, t):
                pe.wait_ge(s_vh, i * NT + t + 1)
                pe.sem_inc(s_hold["pe"], 1)
                pe.wait_ge(s_val, i * NT + t + 1)
                for g, ks in enumerate((range(0, 4), range(4, 8), range(8, 9))):
                    for k in ks:
                        n = k * 128
                        src = val[:, n:n + 128] if n < NS * CG else vh[t % NSLOT][:, n - NS * CG:n - NS * CG + 128]
                        mm = pe.transpose(bank[1 + g][:, (k % 4) * 128:(k % 4 + 1) * 128], src, ident)
                    mm.then_inc(s_vt, 1)
                pe.wait_ge(s_ve, i * (3 * NT) + 3 * t + 3)
                for k in range(KK):
                    mm = pe.matmul(bank[4][:, 0:128], wdcn[:, k, :], valt[:, k, :], start=(k == 0), stop=(k == KK - 1))
                mm.then_inc(s_do, 1)
                pe.wait_ge(s_rt, i * NT + t + 1)
                pe.sem_inc(s_hold["pe"], 1)

            def d_block(i, k, tail):
                if k == 0:
                    if tail:
                        for t in range(NT - NSLOT, NT):
                            back(i - 1, t)
                    for t in range(NSLOT):
                        offsets(i, t)
                        windows(i, t)
                else:
                    for t in range(NSLOT * k, min(NSLOT * (k + 1), NT)):
                        offsets(i, t)
                        back(i, t - NSLOT)
                        windows(i, t)
                last = min(NSLOT * (k + 1), NT)
                pe.wait_ge(s_fl, i * NT + last)
                pe.wait_ge(s_hp, i * (8 * NT) + 8 * last)
                pe.sem_inc(s_hold["pe"], 1)

            def body(xi, di, tail):
                for k in range(9):
                    if di is not None:
                        d_block(di, k, tail)
                    if xi is None:
                        continue
                    if k == 0:
                        x_qkv(xi, range(0, 3))
                    elif k == 1:
                        x_qkv(xi, range(3, NB))
                        x_route(xi)
                    else:
                        x_band(xi, k - 2)
                    if k == 8:
                        x_offsets(xi)

            pe.wait_ge(s_w, 16 * 14)
            pe.wait_ge(s_mz, 1)
            body(0, None, False)
            body(1, 0, False)
            with pe.Fori(2, NIMG) as i:
                body(i, i - 1, True)
            body(None, NIMG - 1, True)
            for t in range(NT - NSLOT, NT):
                back(NIMG - 1, t)

        @block.scalar
        def _(act):
            def table_copies(i, first):
                for r in range(0, NBLK, 2):
                    s = r % NTB
                    if not (first and r < NTB):
                        act.wait_ge(s_tst[s], i * (16 * TB_USES[s]) + 16 * (r // NTB))
                    act.wait_ge(s_tmm, i * NBLK + r + 1)
                    act.activation(tst[s][:], bank[s][:, :].rearrange("p (q g c) -> p g q c", q=4, g=G),
                                   ACT.Copy).then_inc(s_tev[s], 1)

            table_copies(0, True)
            with act.Fori(1, NIMG) as i:
                table_copies(i, False)

            act.wait_ge(s_w, 16 * 14)
            act.wait_ge(s_mz, 1)
            act.mul(col(BQS), col(BQ), SCALE).then_inc(s_setup, 1)
            act.wait_ge(s_setup, 1)

            def x_qkv(i, bands):
                if bands[0] == 0:
                    act.wait_ge(s_xin, i * 16 + 16)
                    act.activation(xpad[:, 2:2 + H, 2:2 + W], xw[:].rearrange("p (h w) -> p h w", w=W),
                                   ACT.Copy).then_inc(s_xc, 1)
                for b in bands:
                    n = i * NB + b + 1
                    act.wait_ge(s_d, n)
                    act.activation(t2[:], t1[:], ACT.Square).then_inc(s_sq, 1)
                    act.wait_ge(s_mm, i * (7 * NB) + 7 * b + 2)
                    act.activation(t2[:], bank[1][:, 0:BAND], ACT.Sqrt, bias=const("eps")).then_inc(s_sd, 1)
                    per = 16 * ((NB + 1 - b % 2) // 2)
                    if not (isinstance(i, int) and i == 0 and b < 2):
                        act.wait_ge(s_qst[b % 2], i * per + 16 * (b // 2))
                        act.wait_ge(s_kst[b % 2], i * per + 16 * (b // 2))
                    act.wait_ge(s_mm, i * (7 * NB) + 7 * b + 3)
                    act.activation(qb[b % 2][:], bank[2][:, 0:BAND], ACT.Identity, bias=col(BQS),
                                   scale=SCALE).then_inc(s_q, 1)
                    act.wait_ge(s_mm, i * (7 * NB) + 7 * b + 4)
                    act.activation(kb[b % 2][:], bank[3][:, 0:BAND], ACT.Identity, bias=col(BK)).then_inc(s_k, 1)
                    act.wait_ge(s_mm, i * (7 * NB) + 7 * b + 5)
                    for r in range(1):
                        act.activation(
                            xpad[:, 2 + b * WS:2 + (b + 1) * WS, 2:2 + W].rearrange("p r (w c) -> p r w c", c=WS),
                            win(bank[4][:, 0:BAND]), ACT.Identity, bias=col(BV)).then_inc(s_vc, 1)

            def x_band(i, b):
                base = i * P2 + b * NWIN

                def exps(j):
                    n = b * NWIN + j
                    act.wait_ge(s_mx, base + j + 1)
                    for h in range(2):
                        ex = act.activation(pr[n % 2][:, h, :], bank[2 + n % 2][:, h * 256:(h + 1) * 256], ACT.Exp,
                                            bias=nmx[n % 2][:, h:h + 1], accum_out=sm[n % 2][:, h:h + 1])
                    ex.then_inc(s_ex, 1)

                def copy_turned(j):
                    n = b * NWIN + j
                    if n >= 2:
                        act.wait_ge(s_pv, i * P2 + n - 1)
                    act.wait_ge(s_tr, base + j + 1)
                    act.activation(pt[n % 2][:].rearrange("p h m q -> p (h m q)"), bank[4 + n % 2][:],
                                   ACT.Copy).then_inc(s_pt, 1)

                for t in range(NWIN + 1):
                    if t < NWIN:
                        exps(t)
                    if t >= 1:
                        copy_turned(t - 1)
                n = i * NB + b + 1
                act.wait_ge(s_d2, n)
                act.activation(t2[:], t1[:], ACT.Square).then_inc(s_sq2, 1)
                act.wait_ge(s_post, i * (7 * NB) + 7 * b + 3)
                act.activation(t2[:], bank[0][:, 0:BAND], ACT.Sqrt, bias=const("eps")).then_inc(s_sd2, 1)
                for m in range(HID):
                    act.wait_ge(s_post, i * (7 * NB) + 7 * b + 4 + m)
                    act.activation(hid[:, m, :], bank[2 + m][:, 0:BAND], ACT.Gelu, bias=col(M1 + m)).then_inc(s_gl, 1)

            def x_offsets(i):
                act.wait_ge(s_gm, i + 1)
                act.activation(pool1[:, 1:2], bank[0][:, 0:1], ACT.Relu)
                act.drain()
                act.activation(pool1[:, 2:3], pool1[:, 1:2], ACT.Exp, scale=-1.0).then_inc(s_ge, 1)
                for b in range(NB):
                    act.wait_ge(s_p5, i * (2 * NB) + 2 * b + 1)
                    act.activation(hid[:, 0, :], bank[0][:, 0:BAND], ACT.Relu).then_inc(s_fa, 1)
                    act.wait_ge(s_p5, i * (2 * NB) + 2 * b + 2)
                    act.activation(rows57(ofp, 1 + SP57, b), bank[1][:, 0:BAND].rearrange("p (r c) -> p r c", c=W),
                                   ACT.Relu).then_inc(s_of, 1)

            def hats(i, t):
                act.wait_ge(s_mb, i * NT + t + 1)
                act.activation(msk[:], msk[:], ACT.Exp, scale=-1.0).then_inc(s_me, 1)
                act.wait_ge(s_hx, i * NT + t + 1)
                act.activation(hxt[:], hxt[:], ACT.Abs)
                act.drain()
                act.activation(hxt[:], hxt[:], ACT.Relu, scale=-1.0, bias=1.0).then_inc(s_h2, 1)
                act.wait_ge(s_wy, i * NT + t + 1)
                act.activation(wy[:], wy[:], ACT.Abs)
                act.drain()
                act.activation(wy[:], wy[:], ACT.Relu, scale=-1.0, bias=1.0).then_inc(s_wy2, 1)

            def copy_hats(i, t):
                for q in range(4):
                    act.wait_ge(s_ht, i * (4 * NT) + 4 * t + q + 1)
                    act.activation(hxs[:, 4 * q:4 * q + 4, :].rearrange("p j n -> p (j n)"), bank[5 + q % 2][:],
                                   ACT.Copy).then_inc(s_hc, 1)

            def back(i, t):
                for g, n in enumerate((4, 4, 1)):
                    act.wait_ge(s_vt, i * (3 * NT) + 3 * t + g + 1)
                    act.activation(valt[:, 4 * g:4 * g + n, :].rearrange("p k q -> p (k q)"),
                                   bank[1 + g][:, 0:n * 128], ACT.Copy).then_inc(s_ve, 1)
                act.wait_ge(s_do, i * NT + t + 1)
                if not (isinstance(i, int) and i == 0 and t == 0):
                    act.wait_ge(s_fin, i * NT + t)
                act.activation(rt[:], bank[4][:, 0:128], ACT.Relu, bias=col(BD)).then_inc(s_rt, 1)

            def d_block(i, k, tail):
                if k == 0:
                    if tail:
                        for t in range(NT - NSLOT, NT):
                            back(i - 1, t)
                    for t in range(NSLOT):
                        hats(i, t)
                        copy_hats(i, t)
                else:
                    for t in range(NSLOT * k, min(NSLOT * (k + 1), NT)):
                        hats(i, t)
                        back(i, t - NSLOT)
                        copy_hats(i, t)

            def body(xi, di, tail):
                for k in range(9):
                    if di is not None:
                        d_block(di, k, tail)
                    if xi is None:
                        continue
                    if k == 0:
                        x_qkv(xi, range(0, 3))
                    elif k == 1:
                        x_qkv(xi, range(3, NB))
                    else:
                        x_band(xi, k - 2)
                    if k == 8:
                        x_offsets(xi)

            body(0, None, False)
            body(1, 0, False)
            with act.Fori(2, NIMG) as i:
                body(i, i - 1, True)
            body(None, NIMG - 1, True)
            for t in range(NT - NSLOT, NT):
                back(NIMG - 1, t)

        @block.vector
        def _(dve):
            for s in range(2):
                dve.memset(src_s[s][:, 0:SW], 0.0)
                z = dve.memset(src_s[s][:, (SH + 1) * SW:], 0.0)
            z.then_inc(s_z, 1)
            dve.memset(rows_s[:], 0.0)
            dve.memset(fpad[:], 0.0)
            dve.drain()
            dve.wait_ge(s_src, 48)
            wres = const("wres")

            for s in range(2):
                src = src_s[s][:].rearrange("p (r c) -> p r c", c=SW)
                for t in range(4):
                    for q in range(8):
                        wt = wres[:, t * H + 7 * q:t * H + 7 * q + 7].unsqueeze(2).to_broadcast([128, 7, SW])
                        o = (rows_s[:, 7 * q:7 * q + 7, 1:1 + SW] if t == 0 else
                             prod_s[:, q * 7 * SW:(q + 1) * 7 * SW].rearrange("p (r c) -> p r c", c=SW))
                        dve.tensor_tensor(o, src[:, 8 * q + t:8 * q + t + 7, :], wt, ALU.mult)
                    dve.drain()
                    if t:
                        o = rows_s[:, :, 1:1 + SW]
                        dve.tensor_tensor(o, o, prod_s[:].rearrange("p (r c) -> p r c", c=SW), ALU.add)
                        dve.drain()
                pv = prod_s[:, 0:PIX].rearrange("p (r c) -> p r c", c=W)
                for t in range(4):
                    for q in range(8):
                        wt = wres[:, t * H + 7 * q:t * H + 7 * q + 7].unsqueeze(1).to_broadcast([128, H, 7])
                        o = (up_s[s][:] if t == 0 else pv)[:, :, 7 * q:7 * q + 7]
                        dve.tensor_tensor(o, rows_s[:, :, 8 * q + t:8 * q + t + 7], wt, ALU.mult)
                    dve.drain()
                    if t:
                        dve.tensor_tensor(up_s[s][:], up_s[s][:], pv, ALU.add)
                        dve.drain()

            fp = fpad[:, 0:TS_ * TS_].rearrange("p (r c) -> p r c", c=TS_)[:, 1:1 + H, 1:1 + W]
            wbat = const("wbat")

            def table_image(i, first):
                if not first:
                    dve.wait_ge(s_tmm, i * NBLK)
                dve.tensor_copy(bcol[:], wbat[:, bass.ds(i * 2, 2)])
                dve.drain()
                dve.tensor_scalar(fp, up_s[0][:], bcol[:, 0:1], None, ALU.mult)
                dve.drain()
                dve.scalar_tensor_tensor(out=fp, in0=up_s[1][:], scalar=bcol[:, 1:2], in1=fp,
                                         op0=ALU.mult, op1=ALU.add)
                dve.drain()
                if not first:
                    dve.wait_ge(s_fst, i * 16)
                dve.tensor_scalar(fdense[:].rearrange("p (r c) -> p r c", c=W), fp, 2.0, None,
                                  ALU.mult).then_inc(s_up, 1)
                for r in range(1, NBLK, 2):
                    s = r % NTB
                    if not (first and r < NTB):
                        dve.wait_ge(s_tst[s], i * (16 * TB_USES[s]) + 16 * (r // NTB))
                    dve.wait_ge(s_tmm, i * NBLK + r + 1)
                    dve.tensor_copy(tst[s][:], bank[s][:, :].rearrange("p (q g c) -> p g q c", q=4, g=G)
                                    ).then_inc(s_tev[s], 1)

            table_image(0, True)
            with dve.Fori(1, NIMG) as i:
                table_image(i, False)

            dve.wait_ge(s_fst, 16 * NIMG)
            for s in range(NTB):
                dve.wait_ge(s_tst[s], 16 * NIMG * TB_USES[s])
            dve.wait_ge(s_w, 16 * 14)
            dve.memset(xpad[:], 0.0)
            dve.memset(qbd[:], 0.0)
            dve.memset(ofp[:], 0.0)
            dve.memset(xd[:], 0.0)
            dve.memset(fx[:], 0.0)
            for s in range(2):
                dve.memset(osb[s][:], 0.0)
            dve.tensor_tensor(kyxb[:], bom[:, 0:2 * S], const("kyx"), ALU.add).then_inc(s_mz, 1)

            def x_pos(i):
                xv = xw[:].rearrange("p (h w) -> p h w", w=W)
                dve.wait_ge(s_xc, i + 1)
                dve.tensor_scalar(xw[:], xw[:], col(POSB), None, ALU.add)
                for k in range(9):
                    dve.drain()
                    y, x = k // 3, k % 3
                    last = dve.scalar_tensor_tensor(out=xv, in0=xpad[:, 1 + y:1 + y + H, 1 + x:1 + x + W],
                                                    scalar=posw[:, k:k + 1], in1=xv, op0=ALU.mult, op1=ALU.add)
                last.then_inc(s_xpos, 1)

            def x_qkv(i, bands):
                if bands[0] == 0:
                    x_pos(i)
                for b in bands:
                    n = i * NB + b + 1
                    mm = i * (7 * NB) + 7 * b
                    dve.wait_ge(s_mm, mm + 1)
                    dve.tensor_tensor(t1[:], band(xw, b), bank[0][:, 0:BAND], ALU.subtract).then_inc(s_d, 1)
                    dve.wait_ge(s_sd, n)
                    dve.reciprocal(t2[:], t2[:])
                    dve.drain()
                    dve.tensor_tensor(t1[:], t1[:], t2[:], ALU.mult)
                    dve.drain()
                    dve.tensor_scalar(win(yw[:]), img(b)(t1[:]), col(G1), col(B1), ALU.mult, ALU.add).then_inc(s_y, 1)
                    for m in range(2):
                        j0, j1 = 4 * m, min(4 * m + 4, NWIN)
                        if m == 0 and not (isinstance(i, int) and i == 0 and b == 0):
                            dve.wait_ge(s_vst, i * (16 * NB) + 16 * b)
                        dve.wait_ge(s_mm, mm + 6 + m)
                        last = dve.tensor_tensor(
                            vb[:, j0:j1, :], bank[5 + m][0:64, 0:(j1 - j0) * C].rearrange("p (w c) -> p w c", c=C),
                            bvrow[:].unsqueeze(1).to_broadcast([64, j1 - j0, C]), ALU.add)
                    last.then_inc(s_v, 1)
                    if b == bands[-1]:
                        dve.wait_ge(s_vc, n)
                    dve.wait_ge(s_k, n)
                    dve.tensor_reduce(qm[:, b * NWIN:(b + 1) * NWIN], qb[b % 2][:].rearrange("p (w n) -> p w n", n=W2),
                                      AX.X, ALU.add)
                    dve.tensor_reduce(km[:, b * NWIN:(b + 1) * NWIN], kb[b % 2][:].rearrange("p (w n) -> p w n", n=W2),
                                      AX.X, ALU.add).then_inc(s_qm, 1)

            def x_route(i):
                dve.wait_ge(s_lg, i + 1)
                dve.tensor_scalar(lg[0:P2, :], bank[7][0:P2, 0:P2], 1.0 / (W2 * W2), None, ALU.mult)
                dve.drain()
                dve.max(mx8[0:P2, :], lg[0:P2, :])
                dve.drain()
                dve.max_index(ix8[0:P2, :], mx8[0:P2, :], lg[0:P2, :]).then_inc(s_ix, 1)

            def x_band(i, b):
                base = i * P2 + b * NWIN
                olv = ol[:].rearrange("p (r c) -> p r c", c=W)

                def lepe(k):
                    y, x = k // 5, k % 5
                    v = xpad[:, b * WS + y:b * WS + y + WS, x:x + W]
                    if k == 0:
                        dve.tensor_scalar(olv, v, lepw[:, 0:1], col(LB), ALU.mult, ALU.add)
                    else:
                        dve.drain()
                        dve.scalar_tensor_tensor(out=olv, in0=v, scalar=lepw[:, k:k + 1], in1=olv,
                                                 op0=ALU.mult, op1=ALU.add)

                def maxes(j):
                    n = b * NWIN + j
                    dve.wait_ge(s_sc, base + j + 1)
                    dve.tensor_reduce(nmx[n % 2][:], bank[2 + n % 2][:].rearrange("p (h k) -> p h k", h=2),
                                      AX.X, ALU.max, negate=True).then_inc(s_mx, 1)

                def scale_heads(j):
                    n = b * NWIN + j
                    dve.wait_ge(s_ex, base + j + 1)
                    dve.reciprocal(rinv[:], sm[n % 2][:])
                    dve.drain()
                    dve.wait_ge(s_pv, base + j + 1)
                    for g in range(2):
                        q = slice(64 * g, 64 * g + 64)
                        o = osb[n % 2][q, :].rearrange("p (h g d) -> p h g d", h=2, g=2)[:, :, g, :]
                        x = bank[6][q, 0:2 * C].rearrange("p (h x d) -> p h x d", h=2, x=4)
                        for h in range(2):
                            last = dve.tensor_scalar(o[:, h, :], x[:, h, 2 * h + g, :], rinv[q, h:h + 1], None, ALU.mult)
                    last.then_inc(s_os, 1)

                taps = iter(range(25))
                for t in range(NWIN + 2):
                    if 0 <= t - 2 < NWIN:
                        scale_heads(t - 2)
                    if t < NWIN:
                        maxes(t)
                    if t == 0:
                        dve.wait_ge(s_vc, i * NB + NB)
                    for k in range(3 * t, min(3 * t + 3, 25)):
                        lepe(k)
                dve.drain()
                dve.wait_ge(s_ot, i * NB + b + 1)
                olr = img(b)(ol[:])
                dve.tensor_tensor(olr, olr, win(bank[7][:, 0:BAND]), ALU.add).then_inc(s_ol, 1)
                n = i * NB + b + 1
                post = i * (7 * NB) + 7 * b
                dve.wait_ge(s_post, post + 1)
                dve.scalar_tensor_tensor(out=band(xw, b), in0=bank[0][:, 0:BAND], scalar=col(BO), in1=band(xw, b),
                                         op0=ALU.add, op1=ALU.add).then_inc(s_xa, 1)
                dve.drain()
                dve.wait_ge(s_post, post + 2)
                dve.tensor_tensor(t1[:], band(xw, b), bank[1][:, 0:BAND], ALU.subtract).then_inc(s_d2, 1)
                dve.wait_ge(s_sd2, n)
                dve.reciprocal(t2[:], t2[:])
                dve.drain()
                dve.tensor_tensor(t1[:], t1[:], t2[:], ALU.mult)
                dve.drain()
                dve.tensor_scalar(yw[:], t1[:], col(G2), col(B2), ALU.mult, ALU.add).then_inc(s_z2, 1)
                dve.wait_ge(s_post, post + 7)
                dve.scalar_tensor_tensor(out=band(xw, b), in0=bank[5][:, 0:BAND], scalar=col(M2), in1=band(xw, b),
                                         op0=ALU.add, op1=ALU.add).then_inc(s_xm, 1)

            def x_offsets(i):
                dve.drain()
                dve.tensor_reduce(pool1[:, 3:4], xw[:], AX.X, ALU.add)
                dve.drain()
                dve.tensor_scalar(pool1[:, 0:1], pool1[:, 3:4], 1.0 / PIX, None, ALU.mult).then_inc(s_pl, 1)
                dve.wait_ge(s_ge, i + 1)
                dve.tensor_scalar(pool1[:, 2:3], pool1[:, 2:3], 1.0, None, ALU.add)
                dve.drain()
                dve.reciprocal(pool1[:, 3:4], pool1[:, 2:3])
                dve.drain()
                dve.tensor_scalar(pool1[:, 3:4], pool1[:, 3:4], 1.0, None, ALU.add)
                dve.drain()
                for b in range(NB):
                    if b:
                        dve.wait_ge(s_p5, i * (2 * NB) + 2 * b - 1)
                    dve.tensor_scalar(t1[:], band(xw, b), pool1[:, 3:4], None, ALU.mult).then_inc(s_fi, 1)

            def positions(i, t):
                dve.wait_ge(s_om, i * NT + t + 1)
                dve.tensor_tensor(msk[:], bank[0][:, 2 * S:3 * S], bom[:, 2 * S:3 * S], ALU.add).then_inc(s_mb, 1)
                dve.tensor_tensor(tmp[:], bank[0][:, 0:2 * S], kyxb[:], ALU.add)
                dve.drain()
                dve.tensor_scalar(pyx[:, 0:S], tmp[:, 0:S], const("posy")[:, t:t + 1], -1.0, ALU.add, ALU.max)
                dve.tensor_scalar(pyx[:, S:], tmp[:, S:], const("posx")[:, t:t + 1], -1.0, ALU.add, ALU.max)
                dve.drain()
                dve.tensor_scalar(pyx[:], pyx[:], float(H), None, ALU.min)
                dve.drain()
                dve.tensor_tensor(hxt[:], pyx[:, S + NS:].unsqueeze(2).to_broadcast([128, NH, XP]),
                                  const("iota").unsqueeze(1).to_broadcast([128, NH, XP]), ALU.subtract).then_inc(s_hx, 1)
                dve.tensor_scalar(pyr[:], pyx[:, NS:S], -float(t * 128 // SP57), None, ALU.add)
                dve.drain()
                dve.tensor_tensor(wy[:], pyr[:].unsqueeze(2).to_broadcast([128, NH, WR]),
                                  const("rowk").rearrange("p (h r) -> p h r", r=WR), ALU.subtract)
                dve.drain()
                dve.tensor_scalar(vio[:], wy[:, :, 0], -(WR - 1) / 2, None, ALU.add).then_inc(s_wy, 1)
                dve.drain()
                dve.tensor_reduce(vmx[:, 0:1], vio[:], AX.X, ALU.max, apply_absolute_value=True)
                dve.drain()
                dve.tensor_scalar(vmx[:, 1:2], vmx[:, 0:1], (WR - 1) / 2, None, ALU.is_gt).then_inc(s_vm, 1)

            def indices(i, t):
                s = t % NSLOT
                dve.tensor_scalar(fl[:], pyx[:], MAGIC, None, ALU.add)
                dve.drain()
                dve.tensor_scalar(fl[:], fl[:], -MAGIC, None, ALU.add)
                dve.drain()
                dve.tensor_tensor(tmp[:], fl[:], pyx[:], ALU.is_gt)
                dve.drain()
                dve.tensor_tensor(fl[:], fl[:], tmp[:], ALU.subtract)
                dve.drain()
                dve.scalar_tensor_tensor(out=tmp[:, 0:S], in0=fl[:, 0:S], scalar=float(TS_), in1=fl[:, S:],
                                         op0=ALU.mult, op1=ALU.add)
                dve.tensor_tensor(pyx[:], pyx[:], fl[:], ALU.subtract)
                dve.drain()
                dve.scalar_tensor_tensor(out=idx[s][:], in0=tmp[:, 0:S], scalar=float(G), in1=gimg[:],
                                         op0=ALU.mult, op1=ALU.add).then_inc(s_ir, 1)
                dve.wait_ge(s_me, i * NT + t + 1)
                dve.tensor_scalar(msk[:], msk[:], 1.0, None, ALU.add)
                dve.drain()
                dve.reciprocal(msk[:], msk[:])
                dve.drain()
                dve.tensor_tensor(ady[:, :, 1], pyx[:, 0:S], msk[:], ALU.mult)
                dve.drain()
                dve.tensor_tensor(ady[:, :, 0], msk[:], ady[:, :, 1], ALU.subtract)
                dve.drain()
                dve.tensor_tensor(wts[s][:, :, :, 1], ady[:], pyx[:, S:].unsqueeze(2).to_broadcast([128, S, 2]), ALU.mult)
                dve.drain()
                dve.tensor_tensor(wts[s][:, :, :, 0], ady[:], wts[s][:, :, :, 1], ALU.subtract)
                dve.wait_ge(s_wy2, i * NT + t + 1)
                dve.tensor_tensor(wy[:], wy[:], msk[:, NS:].unsqueeze(2).to_broadcast([128, NH, WR]), ALU.mult)
                dve.wait_ge(s_fm, i * NT + t + 1)
                if not (isinstance(i, int) and i == 0):
                    dve.wait_ge(s_fbd, i * NT + t + 1 - NT)
                dve.tensor_scalar(flag[0:1, t:t + 1], bank[0][0:1, 0:1], 0.0, None, ALU.is_gt).then_inc(s_fl, 1)
                dve.drain()

            def weigh_windows(i, t):
                v = vh[t % NSLOT][:].rearrange("p (q j a c) -> p q a j c", q=4, j=4, a=2)
                w = wy[:].rearrange("p (q j a) r -> p q a j r", q=4, j=4)
                for q in range(4):
                    for a in range(2):
                        n = 2 * q + a
                        dve.wait_ge(s_hm, i * (8 * NT) + 8 * t + n + 1)
                        dve.tensor_tensor(
                            prod[:], bank[1 + 2 * (q % 2) + a][:].rearrange("p (j r c) -> p j r c", j=4, r=WR),
                            w[:, q, a].unsqueeze(3).to_broadcast([128, 4, WR, CG]), ALU.mult).then_inc(s_hp, 1)
                        dve.drain()
                        dve.tensor_reduce(v[:, q, a], prod[:].rearrange("p j r c -> p j c r"), AX.X, ALU.add)
                        dve.drain()

            def back(i, t):
                s = t % NSLOT
                n = i * NT + t + 1
                g = gbuf[s][:].rearrange("p s y x c -> p (s y x) c")
                w = wts[s][:].rearrange("p s y x -> p (s y x)")
                dve.drain()
                dve.wait_ge(s_gs, n)
                dve.sem_inc(s_hold["dve"], 1)
                dve.wait_ge(s_g[s], 16 * NS)
                dve.tensor_tensor(g, g, w[:, 0:4 * NS].unsqueeze(2).to_broadcast([128, 4 * NS, CG]), ALU.mult)
                dve.drain()
                dy = [gbuf[s][:, :, y].rearrange("p s x c -> p s (x c)") for y in range(2)]
                dve.tensor_tensor(dy[0], dy[0], dy[1], ALU.add)
                dve.drain()
                if not (isinstance(i, int) and i == 0 and t == 0):
                    dve.wait_ge(s_vt, i * (3 * NT) + 3 * t)
                dve.tensor_tensor(val[:].rearrange("p (s c) -> p s c", c=CG), gbuf[s][:, :, 0, 0, :],
                                  gbuf[s][:, :, 0, 1, :], ALU.add).then_inc(s_val, 1)

            def general(i, t):
                s = t % NSLOT
                w = wts[s][:].rearrange("p s y x -> p (s y x)")
                f = dve.value_load(flag[0:1, t:t + 1], min_val=0, max_val=1)
                with dve.If(f > 0):
                    dve.drain()
                    dve.wait_ge(s_fbd, i * NT + t + 1)
                    dve.sem_inc(s_hold["dve"], 1)
                    p3 = hxt[:].rearrange("p h (q c) -> p (h q) c", c=CG)
                    dve.tensor_tensor(p3, p3, w[:, 4 * NS:].unsqueeze(2).to_broadcast([128, 4 * NH, CG]), ALU.mult)
                    dve.drain()
                    dve.tensor_tensor(hxt[:, :, 0:2 * CG], hxt[:, :, 0:2 * CG], hxt[:, :, 2 * CG:], ALU.add)
                    dve.drain()
                    dve.tensor_tensor(vh[s][:].rearrange("p (h c) -> p h c", c=CG), hxt[:, :, 0:CG],
                                      hxt[:, :, CG:2 * CG], ALU.add)
                dve.drain().then_inc(s_vh, 1)

            def finish(i, t):
                dve.wait_ge(s_rt, i * NT + t + 1)
                x = xd[:, t * 128:(t + 1) * 128]
                dve.tensor_tensor(x, x, rt[:], ALU.add).then_inc(s_fin, 1)

            def hand_over(i, tail):
                if tail:
                    dve.wait_ge(s_out, i * 16)
                dve.tensor_copy(xd[:, 0:H * SP57].rearrange("p (h w) -> p h w", w=SP57)[:, :, 0:W],
                                xw[:].rearrange("p (h w) -> p h w", w=W)).then_inc(s_xd, 1)

            def d_block(i, k, tail):
                if k == 0:
                    if tail:
                        for t in range(NT - NSLOT, NT):
                            general(i - 1, t)
                            back(i - 1, t)
                            finish(i - 1, t)
                    dve.tensor_scalar(gimg[:], const("gidx"), const("ibase")[:, bass.ds(i, 1)], None, ALU.add)
                    dve.drain()
                    for t in range(NSLOT):
                        positions(i, t)
                        indices(i, t)
                        weigh_windows(i, t)
                    hand_over(i, tail)
                else:
                    for t in range(NSLOT * k, min(NSLOT * (k + 1), NT)):
                        general(i, t - NSLOT)
                        positions(i, t)
                        back(i, t - NSLOT)
                        indices(i, t)
                        finish(i, t - NSLOT)
                        weigh_windows(i, t)

            def body(xi, di, tail):
                for k in range(9):
                    if di is not None:
                        d_block(di, k, tail)
                    if xi is None:
                        continue
                    if k == 0:
                        x_qkv(xi, range(0, 3))
                    elif k == 1:
                        x_qkv(xi, range(3, NB))
                        x_route(xi)
                    else:
                        x_band(xi, k - 2)
                    if k == 8:
                        x_offsets(xi)

            body(0, None, False)
            body(1, 0, False)
            with dve.Fori(2, NIMG) as i:
                body(i, i - 1, True)
            body(None, NIMG - 1, True)
            for t in range(NT - NSLOT, NT):
                general(NIMG - 1, t)
                back(NIMG - 1, t)
                finish(NIMG - 1, t)


def kernel(**inputs):
    import concourse.bacc as bacc
    from concourse.bass_utils import run_bass_kernel_spmd

    v = {k: np.asarray(x) for k, x in inputs.items()}
    om = v["L1_conv_w_offmask"].reshape(3 * S, C, KK)
    order = np.array([(g * KK + k) * 2 + d for d in range(2) for g, k in ORDER] + [2 * S + g * KK + k for g, k in ORDER])
    qkv_b = v["L0_conv_qkv_b"]
    m1 = v["L0_conv_mlp_b1"]
    dcn = v["L1_conv_w_dcn"].reshape(C, C, KK).transpose(1, 2, 0)
    arrays = {
        "x": v["x"].reshape(B, C, PIX),
        "feat_s": v["L1_conv_feat_s"].reshape(2, C, SH * SW),
        "consts": constants(),
        "qkv_w": v["L0_conv_qkv_w"], "wo_w": v["L0_conv_wo_w"],
        "mlp_w1": v["L0_conv_mlp_w1"], "mlp_w2": v["L0_conv_mlp_w2"],
        "w_fsm_t": v["L1_conv_w_fsm"].T, "w_atten_t": v["L1_conv_w_atten"].T, "w_off_t": v["L1_conv_w_off"].T,
        "w_om_t": om[order].transpose(1, 2, 0),
        "w_dcn_t": np.stack([dcn[g * CG:(g + 1) * CG, k] for g, k in ORDER]).reshape(KK, 128, C).transpose(1, 0, 2),
        "pos_w": v["L0_conv_pos_w"].reshape(C, 9), "lepe_w": v["L0_conv_lepe_w"].reshape(C, 25),
        "cols": np.stack([v["L0_conv_pos_b"], v["L0_conv_ln1_g"], v["L0_conv_ln1_b"], qkv_b[0:C], qkv_b[C:2 * C],
                          qkv_b[2 * C:], v["L0_conv_lepe_b"], v["L0_conv_wo_b"], v["L0_conv_ln2_g"],
                          v["L0_conv_ln2_b"], v["L0_conv_mlp_b2"], v["L1_conv_b_dcn"],
                          m1[0:C], m1[C:2 * C], m1[2 * C:]], axis=1),
        "bv": qkv_b[2 * C:],
        "b_om": v["L1_conv_b_offmask"][order],
    }
    arrays = {k: np.ascontiguousarray(x) for k, x in arrays.items()}
    nc = bacc.Bacc("TRN2", target_bir_lowering=False, num_devices=1)
    aps = {k: nc.dram_tensor("in_" + k, x.shape, mybir.dt.from_np(x.dtype), kind="ExternalInput").ap()
           for k, x in arrays.items()}
    out = nc.dram_tensor("out", (B, C, H, W), F32, kind="ExternalOutput").ap()
    build(nc, aps, out)
    r = run_bass_kernel_spmd(nc, [{"in_" + k: x for k, x in arrays.items()}], core_ids=[0])
    return r.results[0]["out"]
```

```python
from contextlib import ExitStack

import numpy as np

import concourse.bass as bass
from concourse import mybir

F32 = mybir.dt.float32
U32 = mybir.dt.uint32
ALU = mybir.AluOpType
ACT = mybir.ActivationFunctionType
AX = mybir.AxisListType

B, C, H, W = 16, 128, 56, 56
NIMG = B
PIX = H * W
HEADS, HD, NWIN, WS, TOPK = 4, 32, 7, 8, 4
P2, W2 = NWIN * NWIN, WS * WS
BAND = WS * W
NB = NWIN
HID = 3
SCALE = float(C) ** -0.5
SH, SW = 64, 64
G, KK, CG = 8, 9, 16
S = G * KK
TS_ = W + 2
NBLK = -(-TS_ * TS_ // 128)
TROWS = NBLK * 128 * G
FPAD = NBLK * 128 + TS_ + 1
PATCH = 4 * CG
SP57 = W + 1
NT = 25
POS = NT * 128
OFLEN = 1 + SP57 + POS + SP57 + 1
MAGIC = 12582912.0
NSLOT = 3
NVH = NSLOT + 1
NH = 32
NS = S - NH
WR = 8
WUP = 2
XP = 64
FROW = 1 + WUP
NROWS = (NT * 128 - 1 - 8) // SP57 + WR + 2


def window_rows(t):
    return WR if t * 128 % SP57 + 127 >= 3 * SP57 else WR - 1


_ALL = [(g, k) for g in range(G) for k in range(KK)]
ORDER = _ALL[NH:] + _ALL[:NH]
GH = _ALL[NH - 1][0] + 1
SLOT_USES = [len(range(s, NT, NSLOT)) for s in range(NSLOT)]
NKV = 6
KV_USES = [len(range(s, P2, NKV)) for s in range(NKV)]
EARLY = (3, 6)
NTB = 4
TB_USES = [len(range(s, NBLK, NTB)) for s in range(NTB)]

CONSTS = {}


def const_layout():
    at = 0
    for name, n in (("ident", 128), ("fold", 64), ("mean", 128), ("posy", NT), ("posx", NT), ("kyx", 2 * S),
                    ("gidx", S), ("ibase", B), ("rowk", NH * WR), ("iota", XP), ("wres", 4 * H), ("wbat", 2 * B), ("eps", 1)):
        CONSTS[name] = (at, n)
        at += n
    return at


NCONST = const_layout()


def resize_matrix(n_in, n_out):
    inv = np.float32(n_in / n_out)
    kscale = max(inv, np.float32(1.0))
    at = (np.arange(n_out, dtype=np.float32) + np.float32(0.5)) * inv - np.float32(0.5)
    x = np.abs(at[None, :] - np.arange(n_in, dtype=np.float32)[:, None]) / kscale
    w = np.maximum(np.float32(0), np.float32(1) - x)
    return (w / w.sum(0, keepdims=True)).astype(np.float32)


def constants():
    c = np.zeros((128, NCONST), np.float32)

    def put(name, v):
        a, n = CONSTS[name]
        c[:, a:a + n] = v

    put("ident", np.eye(128))
    put("fold", np.concatenate([np.eye(64), np.eye(64)], 0))
    put("mean", 1.0 / C)
    pos = np.arange(NT)[None, :] * 128 + np.arange(128)[:, None]
    put("posy", pos // SP57)
    put("posx", pos % SP57)
    k = np.array([k for _, k in ORDER])
    put("kyx", np.concatenate([k // 3 - 1, k % 3 - 1])[None])
    put("gidx", (np.array([g for g, _ in ORDER]) + (TS_ + 1) * G)[None])
    put("rowk", (k[NS:, None] // 3 - 1 - WUP + np.arange(WR)).reshape(1, -1))
    put("iota", np.arange(XP)[None])
    put("ibase", (np.arange(B) * TROWS)[None])
    m = resize_matrix(SH, H)
    wres = np.zeros((4, H), np.float32)
    for y in range(H):
        for t in range(4):
            src = 8 * (y // 7) + y % 7 + t - 1
            if 0 <= src < SH:
                wres[t, y] = m[src, y]
    put("wres", wres.reshape(1, -1))
    mb = resize_matrix(2, B)
    put("wbat", mb.T.reshape(1, -1))
    put("eps", 1e-6)
    return c


def build(nc, a, out):
    table = nc.dram_tensor("patch_table", (NIMG * TROWS, PATCH), F32, kind="Internal").ap()
    fup = nc.dram_tensor("feat_up_twice", (NIMG, C, PIX), F32, kind="Internal").ap()
    qd = nc.dram_tensor("q_windows", (P2, C, W2), F32, kind="Internal").ap()
    kd = nc.dram_tensor("k_windows", (P2, C, W2), F32, kind="Internal").ap()
    vd = nc.dram_tensor("v_windows", (P2, W2, C), F32, kind="Internal").ap()

    with ExitStack() as ctx:
        def sb(name, shape, dt=F32, c=ctx):
            return c.enter_context(nc.sbuf_tensor(name, shape, dt))

        def sem(name):
            return ctx.enter_context(nc.semaphore(name))

        bank = [ctx.enter_context(nc.psum_tensor(f"bank{n}", [128, 512], F32)) for n in range(8)]
        cst = sb("cst", [128, NCONST])

        def const(name):
            at, n = CONSTS[name]
            return cst[:, at:at + n]

        tctx = ExitStack()
        src_s = [sb(f"src{s}", [128, (SH + 2) * SW], c=tctx) for s in range(2)]
        rows_s = sb("rows_s", [128, H, SW + 2], c=tctx)
        prod_s = sb("prod_s", [128, H * SW], c=tctx)
        up_s = [sb(f"up{s}", [128, H, W], c=tctx) for s in range(2)]
        fpad = sb("fpad", [128, FPAD], c=tctx)
        fdense = sb("fdense", [128, PIX], c=tctx)
        bcol = sb("bcol", [128, 2], c=tctx)
        tst = [sb(f"tst{s}", [128, G, 4, CG], c=tctx) for s in range(NTB)]
        tctx.close()

        wqkv = sb("wqkv", [128, 3 * C])
        wo = sb("wo", [128, C])
        w1 = sb("w1", [128, HID * C])
        w2 = sb("w2", [128, HID, C])
        wfsm = sb("wfsm", [128, C])
        watt = sb("watt", [128, C])
        woff = sb("woff", [128, 2, C])
        wom = sb("wom", [128, KK, 3 * S])
        wdcn = sb("wdcn", [128, KK, C])
        posw = sb("posw", [128, 9])
        lepw = sb("lepw", [128, 25])
        cols = sb("cols", [128, 16])
        POSB, G1, B1, BQ, BK, BV, LB, BO, G2, B2, M2, BD, M1, BQS = 0, 1, 2, 3, 4, 5, 6, 7, 8, 9, 10, 11, 12, 15
        bvrow = sb("bvrow", [64, C])
        bom = sb("bom", [128, 3 * S])
        kyxb = sb("kyxb", [128, 2 * S])
        gimg = sb("gimg", [128, S])

        def col(n):
            return cols[:, n:n + 1]

        xpad = sb("xpad", [128, H + 4, W + 4])
        xw = sb("xw", [128, PIX])
        t1 = sb("t1", [128, BAND])
        t2 = sb("t2", [128, BAND])
        yw = sb("yw", [128, BAND])
        qctx = ExitStack()
        qb = [sb(f"qb{s}", [128, BAND], c=qctx) for s in range(2)]
        kb = [sb(f"kb{s}", [128, BAND], c=qctx) for s in range(2)]
        qctx.close()
        pr = [sb(f"pr{s}", [128, 2, TOPK * W2]) for s in range(2)]
        pt = [sb(f"pt{s}", [128, 2, 2, 128]) for s in range(2)]
        vctx = ExitStack()
        vb = sb("vb", [64, NWIN, C], c=vctx)
        vctx.close()
        ol = sb("ol", [128, NWIN * C])[:, 0:BAND]
        qm = sb("qm", [128, P2])
        km = sb("km", [128, P2])
        lg = sb("lg", [64, P2])
        mx8 = sb("mx8", [64, 8])
        ix8 = sb("ix8", [64, 8], U32)
        sel = sb("sel", [1, P2 * TOPK], U32)
        qbd = sb("qbd", [128, NWIN, HEADS, W2])
        ksel = [sb(f"ksel{s}", [128, TOPK * W2]) for s in range(NKV)]
        vsel = [sb(f"vsel{s}", [128, 2, C]) for s in range(NKV)]
        nmx = [sb(f"nmx{s}", [128, 2]) for s in range(2)]
        sm = [sb(f"sm{s}", [128, 2]) for s in range(3)]
        rinv = [sb(f"rinv{s}", [128, 2]) for s in range(2)]
        osb = [sb(f"osb{s}", [128, C]) for s in range(2)]
        hid = sb("hid", [128, HID, BAND])
        pool1 = sb("pool1", [128, 4])

        xd = sb("xd", [128, POS])
        ofp = sb("ofp", [128, OFLEN])
        gbuf = [sb(f"gbuf{s}", [128, NS, 2, 2, CG]) for s in range(NSLOT)]
        wts = [sb(f"wts{s}", [128, S, 2, 2]) for s in range(NSLOT)]
        idx = [sb(f"idx{s}", [128, S], U32) for s in range(NSLOT)]
        pyx = sb("pyx", [128, 2 * S])
        fl = sb("fl", [128, 2 * S])
        tmp = sb("tmp", [128, 2 * S])
        msk = sb("msk", [128, S])
        ady = sb("ady", [128, S, 2])
        val = sb("val", [128, NS * CG])
        hxt = sb("hxt", [128, NH, XP])
        hxs = sb("hxs", [128, NH // 2, 128])
        fx = sb("fx", [128, GH, NROWS, CG])
        pyr = sb("pyr", [128, NH])
        wy = sb("wy", [128, NH, WR])
        prod = sb("prod", [128, 2, 4, WR, CG])
        lastval = prod[:].rearrange("p s j r c -> p (s j r c)")[:, 0:NS * CG]
        vh = [sb(f"vh{s}", [128, NH * CG]) for s in range(NVH)]
        vio = sb("vio", [128, NH])
        vmx = sb("vmx", [128, 2])
        flag = sb("flag", [1, NT], U32)
        valt = hid[:].rearrange("p m n -> p (m n)")[:, 0:KK * 128].rearrange("p (k n) -> p k n", k=KK)
        rt = sb("rt", [128, 128])

        s_w = sem("weights_loaded")
        s_src = sem("small_maps_loaded")
        s_z = sem("table_borders_zeroed")
        s_up = sem("table_image_ready")
        s_tmm = sem("table_block_turned")
        s_tev = [sem(f"table_block_copied{s}") for s in range(NTB)]
        s_tst = [sem(f"table_block_stored{s}") for s in range(NTB)]
        s_fst = sem("feat_up_stored")
        s_mz = sem("main_buffers_zeroed")
        s_setup = sem("bias_constants_ready")
        s_xin = sem("x_loaded")
        s_xc = sem("x_padded")
        s_xpos = sem("pos_conv_done")
        s_mean = sem("mean_matmul")
        s_var = sem("variance_matmul")
        s_mm = sem("qkv_phase_matmul")
        s_d = sem("centred")
        s_sq = sem("squared")
        s_sd = sem("deviation_ready")
        s_y = sem("normed_ready")
        s_q = sem("q_band_ready")
        s_k = sem("k_band_ready")
        s_vc = sem("v_padded")
        s_v = sem("v_band_ready")
        s_qst = [sem(f"q_band_stored{s}") for s in range(2)]
        s_kst = [sem(f"k_band_stored{s}") for s in range(2)]
        s_vst = sem("v_band_stored")
        s_qm = sem("window_means_ready")
        s_lg = sem("logits_ready")
        s_ix = sem("topk_ready")
        s_sel = sem("topk_flat")
        s_qbd = sem("queries_loaded")
        s_kv = [sem(f"kv_selected{s}") for s in range(NKV)]
        s_sc = sem("scores_ready")
        s_mx = sem("max_ready")
        s_ex = sem("probs_ready")
        s_tr = sem("probs_turned")
        s_pt = sem("probs_turned_copied")
        s_pv = sem("pv_ready")
        s_os = sem("heads_scaled")
        s_ot = sem("attention_band_turned")
        s_ol = sem("attention_plus_lepe")
        s_post = sem("post_phase_matmul")
        s_xa = sem("attention_residual")
        s_d2 = sem("centred2")
        s_sq2 = sem("squared2")
        s_sd2 = sem("deviation2_ready")
        s_z2 = sem("normed2_ready")
        s_gl = sem("gelu_ready")
        s_xm = sem("mlp_residual")
        s_pl = sem("pooled")
        s_gm = sem("gate_matmul")
        s_ge = sem("gate_exp")
        s_fi = sem("gated_band")
        s_p5 = sem("feat_arm_matmul")
        s_p6 = sem("offset_feature_matmul")
        s_fa = sem("feat_arm_ready")
        s_ub = [sem(f"feat_up_band_loaded{s}") for s in range(2)]
        s_of = sem("offset_features_ready")
        s_xd = sem("x_handed_over")
        s_om = sem("offsets_matmul")
        s_mb = sem("mask_logits_ready")
        s_me = sem("mask_exp_ready")
        s_ir = sem("indices_ready")
        s_g = [sem(f"gathered{s}") for s in range(NSLOT)]
        s_gs = sem("gather_started")
        s_val = sem("samples_ready")
        s_lval = sem("last_samples_ready")
        s_vt = sem("samples_turned")
        s_ve = sem("samples_turned_copied")
        s_do = sem("deform_matmul")
        s_hx = sem("column_distance_ready")
        s_h2 = sem("column_hats_ready")
        s_wy = sem("row_distance_ready")
        s_wy2 = sem("row_hats_ready")
        s_ht = sem("column_hats_turned")
        s_hc = sem("column_hats_copied")
        s_hm = sem("window_matmul")
        s_hp = sem("window_weighted")
        s_vm = sem("outside_window_found")
        s_fm = sem("outside_window_matmul")
        s_fl = sem("general_path_flag")
        s_fb = sem("general_path_gathered")
        s_fbd = sem("general_path_over")
        s_vh = sem("hat_samples_ready")
        s_fx = sem("map_columns_loaded")
        s_fx2 = sem("map_columns_doubled")
        s_rt = sem("deform_relu")
        s_fin = sem("tile_finished")
        s_out = sem("image_stored")
        s_hold = {e: sem(f"hold_{e}") for e in ("sp", "pool", "pe", "dve")}

        block = ctx.enter_context(nc.Block())

        def hold(eng, name):
            eng.sem_inc(s_hold[name], 1)

        def band(t, b):
            return t[:, b * BAND:(b + 1) * BAND]

        def img(b):
            return lambda t: t.rearrange("p (r w c) -> p r w c", r=WS, c=WS)

        def win(t):
            return t.rearrange("p (w r c) -> p r w c", w=NWIN, c=WS)

        def rows57(t, off, b):
            at = off + b * WS * SP57
            return t[:, at:at + WS * SP57].rearrange("p (r c) -> p r c", c=SP57)[:, :, 0:W]

        def ln_bufs(b):
            return (t1[:], t2[:]) if b % 2 == 0 else (hid[:, 0, :], hid[:, 1, :])

        def arm_buf(b):
            return hid[:, 0, :] if b % 2 == 0 else yw[:]

        @block.sync
        def _(sp):
            loads = [
                (cst[:], a["consts"]), (wqkv[:], a["qkv_w"]), (wo[:], a["wo_w"]), (w1[:], a["mlp_w1"]),
                (w2[:], a["mlp_w2"].rearrange("(k p) o -> p k o", p=128)),
                (wfsm[:], a["w_fsm_t"]), (watt[:], a["w_atten_t"]),
                (woff[:], a["w_off_t"].rearrange("(k p) o -> p k o", p=128)),
                (wom[:], a["w_om_t"]), (wdcn[:], a["w_dcn_t"]),
                (posw[:], a["pos_w"]), (lepw[:], a["lepe_w"]), (cols[:, 0:15], a["cols"]),
                (bvrow[:], a["bv"].partition_broadcast(64)), (bom[:], a["b_om"].partition_broadcast(128)),
            ]
            sp.wait_ge(s_z, 1)
            for s in range(2):
                sp.dma_start(src_s[s][:, SW:SW + SH * SW], a["feat_s"][s]).then_inc(s_src, 16)
            sp.dma_start(cst[:], a["consts"]).then_inc(s_src, 16)

            def table_stores(i, first):
                sp.wait_ge(s_up, i + 1)
                sp.dma_start(fup[bass.ds(i, 1)].rearrange("a p n -> p (a n)"), fdense[:]).then_inc(s_fst, 16)
                for r in range(NBLK):
                    s = r % NTB
                    sp.wait_ge(s_tev[s], i * TB_USES[s] + r // NTB + 1)
                    dst = table[bass.ds(i * TROWS + r * 128 * G, 128 * G)]
                    sp.dma_start(dst.rearrange("(p g) e -> p (g e)", g=G),
                                 tst[s][:].rearrange("p g q c -> p (g q c)")).then_inc(s_tst[s], 16)

            table_stores(0, True)
            with sp.Fori(1, NIMG) as i:
                table_stores(i, False)
            sp.wait_ge(s_fst, 16 * NIMG)
            for s in range(NTB):
                sp.wait_ge(s_tst[s], 16 * NIMG * TB_USES[s])
            for dst, src in loads[1:]:
                sp.dma_start(dst, src).then_inc(s_w, 16)

            def x_qkv(i):
                if not (isinstance(i, int) and i == 0):
                    sp.wait_ge(s_xd, i)
                sp.dma_start(xw[:], a["x"][bass.ds(i, 1)].rearrange("a p n -> p (a n)")).then_inc(s_xin, 16)
                for b in range(NB):
                    w0 = b * NWIN
                    sp.wait_ge(s_q, i * NB + b + 1)
                    sp.dma_start(qd[w0:w0 + NWIN].rearrange("w p n -> p w n"),
                                 qb[b % 2][:].rearrange("p (w n) -> p w n", w=NWIN)).then_inc(s_qst[b % 2], 16)
                    sp.wait_ge(s_k, i * NB + b + 1)
                    sp.dma_start(kd[w0:w0 + NWIN].rearrange("w p n -> p w n"),
                                 kb[b % 2][:].rearrange("p (w n) -> p w n", w=NWIN)).then_inc(s_kst[b % 2], 16)
                    sp.wait_ge(s_v, i * NB + b + 1)
                    sp.dma_start(vd[w0:w0 + NWIN].rearrange("w n c -> n w c"), vb[:]).then_inc(s_vst, 16)

            def x_select(i):
                sp.wait_ge(s_ix, i + 1)
                sp.dma_start(sel[:], ix8[0:P2, 0:TOPK]).then_inc(s_sel, 16)
                for s in range(2):
                    n = (NB + 1 - s) // 2
                    sp.wait_ge(s_qst[s], i * (16 * n) + 16 * n)
                    sp.wait_ge(s_kst[s], i * (16 * n) + 16 * n)
                sp.wait_ge(s_vst, i * (16 * NB) + 16 * NB)
                sp.wait_ge(s_sel, i * 16 + 16)
                hold(sp, "sp")

            def x_band(i, b):
                if b > 0:
                    sp.wait_ge(s_sc, i * P2 + b * NWIN)
                for h in range(HEADS):
                    sp.dma_start(qbd[h * HD:(h + 1) * HD, :, h, :],
                                 qd[b * NWIN:(b + 1) * NWIN, h * HD:(h + 1) * HD].rearrange("w p n -> p w n")
                                 ).then_inc(s_qbd, 16)
                for j in range(NWIN):
                    n = b * NWIN + j
                    s = n % NKV
                    if n >= NKV:
                        sp.wait_ge(s_pv, i * P2 + n - NKV + 1)
                        hold(sp, "sp")
                    for m in range(TOPK):
                        w = sp.value_load(sel[0:1, n * TOPK + m:n * TOPK + m + 1], min_val=0, max_val=P2 - 1)
                        sp.dma_start(ksel[s][:, m * W2:(m + 1) * W2],
                                     kd[bass.ds(w, 1)].rearrange("a p n -> p (a n)")).then_inc(s_kv[s], 16)
                        sp.dma_start(vsel[s][(m % 2) * 64:(m % 2) * 64 + 64, m // 2, :],
                                     vd[bass.ds(w, 1)].rearrange("a n c -> n (a c)")).then_inc(s_kv[s], 16)

            def x_offsets(i):
                for b in range(NB):
                    if b < 2:
                        sp.wait_ge(s_xm, i * NB + NB)
                    else:
                        sp.wait_ge(s_p6, i * NB + b - 1)
                    sp.dma_start(hid[:, 1 + b % 2, :], fup[bass.ds(i, 1), :, b * BAND:(b + 1) * BAND].rearrange(
                        "a p n -> p (a n)")).then_inc(s_ub[b % 2], 16)

            def map_columns(i):
                if not (isinstance(i, int) and i == 0):
                    sp.wait_ge(s_hp, i * (8 * NT))
                t3 = table[bass.ds(i * TROWS, TROWS)].rearrange("(p g) e -> p g e", g=G)
                at = TS_ + 1
                for g in range(GH):
                    src = t3[at:at + H * TS_, g, 0:CG].rearrange("(y x) c -> x y c", x=TS_)[0:W]
                    sp.dma_start(fx[0:W, g, FROW:FROW + H, :], src).then_inc(s_fx, 16)
                sp.wait_ge(s_fx, i * (16 * GH) + 16 * GH)
                sp.dma_start(fx[XP:XP + W].rearrange("p g r c -> p (g r c)"),
                             fx[0:W].rearrange("p g r c -> p (g r c)")).then_inc(s_fx2, 16)

            def store(i):
                sp.wait_ge(s_fin, i * NT + NT)
                sp.dma_start(out[bass.ds(i, 1)].rearrange("a p h w -> p (a h) w"),
                             xd[:, 0:H * SP57].rearrange("p (h w) -> p h w", w=SP57)[:, :, 0:W]
                             ).then_inc(s_out, 16)

            def body(xi, di, tail):
                if tail:
                    store(di - 1)
                if xi is not None:
                    x_qkv(xi)
                    x_select(xi)
                    for b in range(NB):
                        x_band(xi, b)
                    x_offsets(xi)
                    map_columns(xi)

            sp.wait_ge(s_mz, 1)
            body(0, None, False)
            body(1, 0, False)
            with sp.Fori(2, NIMG) as i:
                body(i, i - 1, True)
            body(None, NIMG - 1, True)
            store(NIMG - 1)
            sp.wait_ge(s_out, 16 * NIMG)

        @block.gpsimd
        def _(pool):
            def gathers(i, first):
                for t in range(NT):
                    s = t % NSLOT
                    pool.wait_ge(s_ir, i * NT + t + 1)
                    hold(pool, "pool")
                    if not (first and t < NSLOT):
                        pool.inc_swdge_sem([s_g[s]], [16 * NS], mode="sub")
                    pool.sem_inc(s_gs, 1)
                    for k in range(NS):
                        pool.indirect_dma_start(gbuf[s][:, k].rearrange("p y x c -> p (y x c)"), None, table,
                                                bass.IndirectOffsetOnAxis(ap=idx[s][:, k:k + 1], axis=0)
                                                ).then_inc(s_g[s], 16)
                    if t >= 2:
                        general(i, t - 2)
                general(i, NT - 2)
                general(i, NT - 1)

            def general(i, t):
                pool.wait_ge(s_fl, i * NT + t + 1)
                hold(pool, "pool")
                f = pool.value_load(flag[0:1, t:t + 1], min_val=0, max_val=1)
                with pool.If(f > 0):
                    pool.wait_ge(s_hp, i * (8 * NT) + 8 * min(t + 3, NT))
                    hold(pool, "pool")
                    if not (isinstance(i, int) and i == 0 and t == 0):
                        pool.wait_ge(s_vh, i * NT + t)
                        hold(pool, "pool")
                    for h in range(NH):
                        pool.indirect_dma_start(hxt[:, h, :], None, table,
                                                bass.IndirectOffsetOnAxis(ap=idx[t % NSLOT][:, NS + h:NS + h + 1], axis=0)
                                                ).then_inc(s_fb, 16)
                    pool.wait_ge(s_fb, 16 * NH)
                    hold(pool, "pool")
                    pool.inc_swdge_sem([s_fb], [16 * NH], mode="sub")
                pool.sem_inc(s_fbd, 1)

            gathers(0, True)
            with pool.Fori(1, NIMG) as i:
                gathers(i, False)

        @block.tensor
        def _(pe):
            ident = const("ident")
            def table_turns(i, first):
                pe.wait_ge(s_up, i + 1)
                for r in range(NBLK):
                    s = r % NTB
                    if not (first and r < NTB):
                        pe.wait_ge(s_tev[s], i * TB_USES[s] + r // NTB)
                    for q in range(4):
                        dy, dx = q // 2, q % 2
                        mm = pe.matmul(bank[s][:, q * 128:(q + 1) * 128],
                                       fpad[:, r * 128 + dy * TS_ + dx:(r + 1) * 128 + dy * TS_ + dx], ident,
                                       start=True, stop=True, is_transpose=True)
                    mm.then_inc(s_tmm, 1)

            table_turns(0, True)
            with pe.Fori(1, NIMG) as i:
                table_turns(i, False)

            def x_qkv(i, bands, ahead):
                def mean(b):
                    if b > bands[0]:
                        pe.wait_ge(s_d, i * NB + b)
                    pe.matmul(bank[0][:, 0:BAND], const("mean"), band(xw, b), start=True, stop=True).then_inc(s_mean, 1)

                def variance(b):
                    if b > bands[0]:
                        pe.wait_ge(s_sd, i * NB + b)
                        pe.sem_inc(s_hold["pe"], 1)
                    pe.wait_ge(s_sq, i * NB + b + 1)
                    pe.matmul(bank[1][:, 0:BAND], const("mean"), ln_bufs(b)[1], start=True, stop=True).then_inc(s_var, 1)

                pe.wait_ge(s_xpos, i + 1)
                for b in bands[:2]:
                    mean(b)
                    variance(b)
                for b in bands:
                    if b + 2 in bands:
                        mean(b + 2)
                    if b > bands[0]:
                        pe.wait_ge(s_vc, i * NB + b)
                    pe.wait_ge(s_y, i * NB + b + 1)
                    for m in range(3):
                        pe.matmul(bank[2 + m][:, 0:BAND], wqkv[:, m * C:(m + 1) * C], yw[:],
                                  start=True, stop=True).then_inc(s_mm, 1)
                    for j in range(NWIN):
                        mm = pe.matmul(bank[5 + j // 4][0:64, (j % 4) * C:(j % 4 + 1) * C], yw[:, j * W2:(j + 1) * W2],
                                       wqkv[:, 2 * C:3 * C], start=True, stop=True)
                        if j in (3, NWIN - 1):
                            mm.then_inc(s_mm, 1)
                    if b + 2 in bands:
                        variance(b + 2)
                if ahead is not None:
                    pe.wait_ge(s_d, i * NB + bands[-1] + 1)
                    offsets(*ahead)
                pe.wait_ge(s_qm, i * NB + bands[-1] + 1)
                pe.sem_inc(s_hold["pe"], 1)

            def x_route(i):
                pe.matmul(bank[7][0:P2, 0:P2], qm[:], km[:], start=True, stop=True).then_inc(s_lg, 1)

            def x_band(i, b, ahead):
                base = i * P2 + b * NWIN

                def scores(j):
                    n = b * NWIN + j
                    s = n % NKV
                    if j == 0:
                        pe.wait_ge(s_qbd, i * (64 * NB) + 64 * (b + 1))
                        pe.wait_ge(s_ix, i + 1)
                    pe.wait_ge(s_kv[s], i * (128 * KV_USES[s]) + 128 * (n // NKV + 1))
                    if j >= 2:
                        pe.wait_ge(s_ex, base + j - 1)
                    for h in range(2):
                        mm = pe.matmul(bank[2 + n % 2][:, h * 256:(h + 1) * 256],
                                       qbd[:, j, 2 * h:2 * h + 2, :].rearrange("p h q -> p (h q)"), ksel[s][:],
                                       start=True, stop=True)
                    mm.then_inc(s_sc, 1)

                def turn(j):
                    n = b * NWIN + j
                    pe.wait_ge(s_ex, base + j + 1)
                    for h in range(2):
                        for m in range(2):
                            mm = pe.transpose(bank[4 + n % 2][:, (2 * h + m) * 128:(2 * h + m + 1) * 128],
                                              pr[n % 2][:, h, m * 128:(m + 1) * 128], ident)
                    mm.then_inc(s_tr, 1)

                def pv(j):
                    n = b * NWIN + j
                    pe.wait_ge(s_pt, base + j + 1)
                    if j >= 1:
                        pe.wait_ge(s_os, base + j)
                    for h in range(2):
                        for m in range(2):
                            mm = pe.matmul(bank[6][:, h * W2:(h + 1) * W2], pt[n % 2][:, h, m, :],
                                           vsel[n % NKV][:, m, h * W2:(h + 1) * W2], start=(m == 0), stop=(m == 1))
                    mm.then_inc(s_pv, 1)

                def turn_out(j):
                    n = b * NWIN + j
                    pe.wait_ge(s_os, base + j + 1)
                    mm = pe.matmul(bank[7][:, j * W2:(j + 1) * W2], osb[n % 2][:], const("fold"),
                                   start=True, stop=True)
                    if j == NWIN - 1:
                        mm.then_inc(s_ot, 1)

                for t in range(NWIN + 3):
                    if t < NWIN:
                        scores(t)
                    if 0 <= t - 1 < NWIN:
                        turn(t - 1)
                    if 0 <= t - 2 < NWIN:
                        pv(t - 2)
                    if 0 <= t - 3 < NWIN:
                        turn_out(t - 3)
                n = i * NB + b + 1
                pe.wait_ge(s_ol, n)
                pe.matmul(bank[0][:, 0:BAND], wo[:], ol[:], start=True, stop=True).then_inc(s_post, 1)
                pe.wait_ge(s_xa, n)
                pe.matmul(bank[1][:, 0:BAND], const("mean"), band(xw, b), start=True, stop=True).then_inc(s_post, 1)
                pe.wait_ge(s_sq2, n)
                pe.matmul(bank[0][:, 0:BAND], const("mean"), t2[:], start=True, stop=True).then_inc(s_post, 1)
                if ahead is not None:
                    pe.wait_ge(s_sd2, n)
                    offsets(*ahead)
                pe.wait_ge(s_z2, n)
                for m in range(HID):
                    pe.matmul(bank[2 + m][:, 0:BAND], w1[:, m * C:(m + 1) * C], yw[:],
                              start=True, stop=True).then_inc(s_post, 1)
                for m in range(HID):
                    pe.wait_ge(s_gl, i * (HID * NB) + HID * b + m + 1)
                    mm = pe.matmul(bank[5][:, 0:BAND], w2[:, m, :], hid[:, m, :], start=(m == 0), stop=(m == HID - 1))
                mm.then_inc(s_post, 1)
                pe.wait_ge(s_xm, n)
                pe.sem_inc(s_hold["pe"], 1)

            def x_offsets(i):
                pe.wait_ge(s_pl, i + 1)
                pe.matmul(bank[0][:, 0:1], watt[:], pool1[:, 0:1], start=True, stop=True).then_inc(s_gm, 1)
                def arm(b):
                    pe.wait_ge(s_fi, i * NB + b + 1)
                    if b:
                        pe.wait_ge(s_fa, i * NB + b)
                    pe.matmul(bank[0][:, 0:BAND], wfsm[:], (t1, t2)[b % 2][:], start=True, stop=True).then_inc(s_p5, 1)

                arm(0)
                for b in range(NB):
                    if b + 1 < NB:
                        arm(b + 1)
                    pe.wait_ge(s_fa, i * NB + b + 1)
                    per = 16 * ((NB + 1 - b % 2) // 2)
                    pe.wait_ge(s_ub[b % 2], i * per + 16 * (b // 2 + 1))
                    if b:
                        pe.wait_ge(s_of, i * NB + b)
                        pe.sem_inc(s_hold["pe"], 1)
                    pe.matmul(bank[1][:, 0:BAND], woff[:, 0, :], arm_buf(b), start=True, stop=False)
                    pe.matmul(bank[1][:, 0:BAND], woff[:, 1, :], hid[:, 1 + b % 2, :],
                              start=False, stop=True).then_inc(s_p6, 1)
                pe.wait_ge(s_of, i * NB + NB)
                pe.sem_inc(s_hold["pe"], 1)

            def offsets(i, t):
                pe.wait_ge(s_of, i * NB + NB)
                if t:
                    pe.wait_ge(s_fl, i * NT + t)
                for k in range(KK):
                    at = 1 + SP57 + t * 128 + (k // 3 - 1) * SP57 + k % 3 - 1
                    mm = pe.matmul(bank[0][:, 0:3 * S], ofp[:, at:at + 128], wom[:, k, :],
                                   start=(k == 0), stop=(k == KK - 1))
                mm.then_inc(s_om, 1)

            def find_outside(i, t):
                pe.wait_ge(s_vm, i * NT + t + 1)
                pe.matmul(bank[0][0:1, 0:1], vmx[:, 1:2], const("mean")[:, 0:1], start=True, stop=True).then_inc(s_fm, 1)

            def windows(i, t, before):
                pe.wait_ge(s_h2, i * NT + t + 1)
                for q in range(4):
                    if q >= 2:
                        pe.wait_ge(s_hc, i * (4 * NT) + 4 * t + q - 1)
                    for j in range(4):
                        p = 4 * q + j
                        mm = pe.transpose(bank[5 + q % 2][:, j * 128:(j + 1) * 128],
                                          hxt[:, 2 * p:2 * p + 2, :].rearrange("p a x -> p (a x)"), ident)
                    mm.then_inc(s_ht, 1)
                if before is not None:
                    pe.wait_ge(s_rt, before)
                pe.wait_ge(s_fx, i * (16 * GH) + 16 * GH)
                pe.wait_ge(s_fx2, i * 16 + 16)
                pe.sem_inc(s_hold["pe"], 1)
                y0 = t * 128 // SP57
                for q in range(4):
                    pe.wait_ge(s_hc, i * (4 * NT) + 4 * t + q + 1)
                    if q >= 2:
                        pe.wait_ge(s_hp, i * (8 * NT) + 8 * t + 2 * q - 2)
                    last = [None, None]
                    for j in range(4):
                        for a in range(2):
                            h = 8 * q + 2 * j + a
                            g, k = ORDER[NS + h]
                            row = y0 + k // 3 - 1 - WUP + FROW
                            wr = window_rows(t)
                            last[a] = pe.matmul(bank[1 + 2 * (q % 2) + a][:, j * 128:j * 128 + wr * CG],
                                                hxs[XP * a:XP * a + XP, 4 * q + j, :],
                                                fx[XP * a:XP * a + XP, g, row:row + wr, :].rearrange("p r c -> p (r c)"),
                                                start=True, stop=True)
                    for a in range(2):
                        last[a].then_inc(s_hm, 1)

            def back(i, t):
                pe.wait_ge(s_vh, i * NT + t + 1)
                pe.sem_inc(s_hold["pe"], 1)
                if t < NT - 1:
                    pe.wait_ge(s_val, i * (NT - 1) + t + 1)
                else:
                    pe.wait_ge(s_lval, i + 1)
                samples = val if t < NT - 1 else lastval
                for g, ks in enumerate((range(0, 4), range(4, 8), range(8, 9))):
                    for k in ks:
                        n = k * 128
                        src = samples[:, n:n + 128] if n < NS * CG else vh[t % NVH][:, n - NS * CG:n - NS * CG + 128]
                        mm = pe.transpose(bank[1 + g][:, (k % 4) * 128:(k % 4 + 1) * 128], src, ident)
                    mm.then_inc(s_vt, 1)
                pe.wait_ge(s_ve, i * (3 * NT) + 3 * t + 3)
                for k in range(KK):
                    mm = pe.matmul(bank[4][:, 0:128], wdcn[:, k, :], valt[:, k, :], start=(k == 0), stop=(k == KK - 1))
                mm.then_inc(s_do, 1)

            def d_block(i, k, tail, started):
                tiles = range(NSLOT * k, min(NSLOT * (k + 1), NT))
                if not started:
                    offsets(i, tiles[0])
                for t in tiles:
                    before = None
                    if tail and t == 0:
                        back(i - 1, NT - NVH)
                        find_outside(i, t)
                        for u in range(NT - NVH + 1, NT):
                            pe.wait_ge(s_rt, (i - 1) * NT + u)
                            pe.sem_inc(s_hold["pe"], 1)
                            back(i - 1, u)
                        before = i * NT
                    elif t >= NVH:
                        pe.wait_ge(s_hp, i * (8 * NT) + 8 * t)
                        pe.sem_inc(s_hold["pe"], 1)
                        back(i, t - NVH)
                        before = i * NT + t - NVH + 1
                    if not (tail and t == 0):
                        find_outside(i, t)
                    windows(i, t, before)
                    if t + 1 in tiles:
                        offsets(i, t + 1)
                last = min(NSLOT * (k + 1), NT)
                pe.wait_ge(s_fl, i * NT + last)
                pe.wait_ge(s_hp, i * (8 * NT) + 8 * last)
                pe.sem_inc(s_hold["pe"], 1)

            def body(xi, di, tail):
                for k in range(9):
                    if di is not None:
                        d_block(di, k, tail, xi is not None and k > 0)
                    if xi is None:
                        continue
                    ahead = (di, NSLOT * (k + 1)) if di is not None and k < 8 else None
                    if k == 0:
                        x_qkv(xi, range(0, 3), ahead)
                    elif k == 1:
                        x_qkv(xi, range(3, NB), ahead)
                        x_route(xi)
                    else:
                        x_band(xi, k - 2, ahead)
                    if k == 8:
                        x_offsets(xi)

            pe.wait_ge(s_w, 16 * 14)
            pe.wait_ge(s_mz, 1)
            body(0, None, False)
            body(1, 0, False)
            with pe.Fori(2, NIMG) as i:
                body(i, i - 1, True)
            body(None, NIMG - 1, True)
            for t in range(NT - NVH, NT):
                if t > NT - NVH:
                    pe.wait_ge(s_rt, (NIMG - 1) * NT + t)
                back(NIMG - 1, t)

        @block.scalar
        def _(act):
            def table_copies(i, first):
                for r in range(0, NBLK, 2):
                    s = r % NTB
                    if not (first and r < NTB):
                        act.wait_ge(s_tst[s], i * (16 * TB_USES[s]) + 16 * (r // NTB))
                    act.wait_ge(s_tmm, i * NBLK + r + 1)
                    act.activation(tst[s][:], bank[s][:, :].rearrange("p (q g c) -> p g q c", q=4, g=G),
                                   ACT.Copy).then_inc(s_tev[s], 1)

            table_copies(0, True)
            with act.Fori(1, NIMG) as i:
                table_copies(i, False)

            act.wait_ge(s_w, 16 * 14)
            act.wait_ge(s_mz, 1)
            act.mul(col(BQS), col(BQ), SCALE).then_inc(s_setup, 1)
            act.wait_ge(s_setup, 1)

            def x_qkv(i, bands):
                if bands[0] == 0:
                    act.wait_ge(s_xin, i * 16 + 16)
                    act.activation(xpad[:, 2:2 + H, 2:2 + W], xw[:].rearrange("p (h w) -> p h w", w=W), ACT.Copy)
                    act.drain()
                    act.activation(xw[:], xw[:], ACT.Identity, bias=col(POSB)).then_inc(s_xc, 1)
                def square(b):
                    act.wait_ge(s_d, i * NB + b + 1)
                    act.activation(ln_bufs(b)[1], ln_bufs(b)[0], ACT.Square).then_inc(s_sq, 1)

                def deviation(b):
                    act.wait_ge(s_var, i * NB + b + 1)
                    act.activation(ln_bufs(b)[1], bank[1][:, 0:BAND], ACT.Sqrt, bias=const("eps")).then_inc(s_sd, 1)

                for b in bands[:2]:
                    square(b)
                    deviation(b)
                for b in bands:
                    per = 16 * ((NB + 1 - b % 2) // 2)
                    if not (isinstance(i, int) and i == 0 and b < 2):
                        act.wait_ge(s_qst[b % 2], i * per + 16 * (b // 2))
                        act.wait_ge(s_kst[b % 2], i * per + 16 * (b // 2))
                    act.wait_ge(s_mm, i * (5 * NB) + 5 * b + 1)
                    act.activation(qb[b % 2][:], bank[2][:, 0:BAND], ACT.Identity, bias=col(BQS),
                                   scale=SCALE).then_inc(s_q, 1)
                    act.wait_ge(s_mm, i * (5 * NB) + 5 * b + 2)
                    act.activation(kb[b % 2][:], bank[3][:, 0:BAND], ACT.Identity, bias=col(BK)).then_inc(s_k, 1)
                    act.wait_ge(s_mm, i * (5 * NB) + 5 * b + 3)
                    act.activation(
                        xpad[:, 2 + b * WS:2 + (b + 1) * WS, 2:2 + W].rearrange("p r (w c) -> p r w c", c=WS),
                        win(bank[4][:, 0:BAND]), ACT.Identity, bias=col(BV)).then_inc(s_vc, 1)
                    if b + 2 in bands:
                        square(b + 2)
                        deviation(b + 2)

            def x_band(i, b):
                base = i * P2 + b * NWIN

                def exps(j):
                    n = b * NWIN + j
                    act.wait_ge(s_mx, base + j + 1)
                    for h in range(2):
                        ex = act.activation(pr[n % 2][:, h, :], bank[2 + n % 2][:, h * 256:(h + 1) * 256], ACT.Exp,
                                            bias=nmx[n % 2][:, h:h + 1], accum_out=sm[n % 3][:, h:h + 1])
                    ex.then_inc(s_ex, 1)

                def copy_turned(j):
                    n = b * NWIN + j
                    if n >= 2:
                        act.wait_ge(s_pv, i * P2 + n - 1)
                    act.wait_ge(s_tr, base + j + 1)
                    act.activation(pt[n % 2][:].rearrange("p h m q -> p (h m q)"), bank[4 + n % 2][:],
                                   ACT.Copy).then_inc(s_pt, 1)

                for t in range(NWIN + 1):
                    if t < NWIN:
                        exps(t)
                    if t >= 1:
                        copy_turned(t - 1)
                n = i * NB + b + 1
                act.wait_ge(s_d2, n)
                act.activation(t2[:], t1[:], ACT.Square).then_inc(s_sq2, 1)
                act.wait_ge(s_post, i * (7 * NB) + 7 * b + 3)
                act.activation(t2[:], bank[0][:, 0:BAND], ACT.Sqrt, bias=const("eps")).then_inc(s_sd2, 1)
                for m in range(HID):
                    act.wait_ge(s_post, i * (7 * NB) + 7 * b + 4 + m)
                    act.activation(hid[:, m, :], bank[2 + m][:, 0:BAND], ACT.Gelu, bias=col(M1 + m)).then_inc(s_gl, 1)

            def x_offsets(i):
                act.wait_ge(s_gm, i + 1)
                act.activation(pool1[:, 1:2], bank[0][:, 0:1], ACT.Relu)
                act.drain()
                act.activation(pool1[:, 2:3], pool1[:, 1:2], ACT.Exp, scale=-1.0).then_inc(s_ge, 1)
                def offset_features(b):
                    act.wait_ge(s_p6, i * NB + b + 1)
                    act.activation(rows57(ofp, 1 + SP57, b), bank[1][:, 0:BAND].rearrange("p (r c) -> p r c", c=W),
                                   ACT.Relu).then_inc(s_of, 1)

                for b in range(NB):
                    act.wait_ge(s_p5, i * NB + b + 1)
                    act.activation(arm_buf(b), bank[0][:, 0:BAND], ACT.Relu).then_inc(s_fa, 1)
                    if b:
                        offset_features(b - 1)
                offset_features(NB - 1)

            def hats(i, t):
                act.wait_ge(s_mb, i * NT + t + 1)
                act.activation(msk[:], msk[:], ACT.Exp, scale=-1.0).then_inc(s_me, 1)
                act.wait_ge(s_hx, i * NT + t + 1)
                hx = hxt[:, :, 0:W]
                act.activation(hx, hx, ACT.Abs)
                act.drain()
                act.activation(hx, hx, ACT.Relu, scale=-1.0, bias=1.0).then_inc(s_h2, 1)
                act.wait_ge(s_wy, i * NT + t + 1)
                act.activation(wy[:], wy[:], ACT.Abs)
                act.drain()
                act.activation(wy[:], wy[:], ACT.Relu, scale=-1.0, bias=1.0).then_inc(s_wy2, 1)

            def copy_hats(i, t):
                for q in range(4):
                    act.wait_ge(s_ht, i * (4 * NT) + 4 * t + q + 1)
                    act.activation(hxs[:, 4 * q:4 * q + 4, :].rearrange("p j n -> p (j n)"), bank[5 + q % 2][:],
                                   ACT.Copy).then_inc(s_hc, 1)

            def copy_samples(i, t):
                for g, n in enumerate((4, 4, 1)):
                    act.wait_ge(s_vt, i * (3 * NT) + 3 * t + g + 1)
                    act.activation(valt[:, 4 * g:4 * g + n, :].rearrange("p k q -> p (k q)"),
                                   bank[1 + g][:, 0:n * 128], ACT.Copy).then_inc(s_ve, 1)

            def relu(i, t):
                act.wait_ge(s_do, i * NT + t + 1)
                if not (isinstance(i, int) and i == 0 and t == 0):
                    act.wait_ge(s_fin, i * NT + t)
                act.activation(rt[:], bank[4][:, 0:128], ACT.Relu, bias=col(BD)).then_inc(s_rt, 1)

            def hand_over(i, tail):
                if tail:
                    act.wait_ge(s_out, i * 16)
                act.activation(xd[:, 0:H * SP57].rearrange("p (h w) -> p h w", w=SP57)[:, :, 0:W],
                               xw[:].rearrange("p (h w) -> p h w", w=W), ACT.Copy).then_inc(s_xd, 1)

            def d_block(i, k, tail):
                for t in range(NSLOT * k, min(NSLOT * (k + 1), NT)):
                    if tail and t == 0:
                        copy_samples(i - 1, NT - NVH)
                        relu(i - 1, NT - NVH)
                    elif t >= NVH:
                        copy_samples(i, t - NVH)
                    hats(i, t)
                    if tail and t == 0:
                        for u in range(NT - NVH + 1, NT):
                            copy_samples(i - 1, u)
                            relu(i - 1, u)
                    elif t >= NVH:
                        relu(i, t - NVH)
                    copy_hats(i, t)
                    if t == 1:
                        hand_over(i, tail)

            def body(xi, di, tail):
                for k in range(9):
                    if di is not None:
                        d_block(di, k, tail)
                    if xi is None:
                        continue
                    if k == 0:
                        x_qkv(xi, range(0, 3))
                    elif k == 1:
                        x_qkv(xi, range(3, NB))
                    else:
                        x_band(xi, k - 2)
                    if k == 8:
                        x_offsets(xi)

            body(0, None, False)
            body(1, 0, False)
            with act.Fori(2, NIMG) as i:
                body(i, i - 1, True)
            body(None, NIMG - 1, True)
            for t in range(NT - NVH, NT):
                copy_samples(NIMG - 1, t)
                relu(NIMG - 1, t)

        @block.vector
        def _(dve):
            for s in range(2):
                dve.memset(src_s[s][:, 0:SW], 0.0)
                z = dve.memset(src_s[s][:, (SH + 1) * SW:], 0.0)
            z.then_inc(s_z, 1)
            dve.memset(rows_s[:], 0.0)
            dve.memset(fpad[:], 0.0)
            dve.drain()
            dve.wait_ge(s_src, 48)
            wres = const("wres")

            for s in range(2):
                src = src_s[s][:].rearrange("p (r c) -> p r c", c=SW)
                for t in range(4):
                    for q in range(8):
                        wt = wres[:, t * H + 7 * q:t * H + 7 * q + 7].unsqueeze(2).to_broadcast([128, 7, SW])
                        o = (rows_s[:, 7 * q:7 * q + 7, 1:1 + SW] if t == 0 else
                             prod_s[:, q * 7 * SW:(q + 1) * 7 * SW].rearrange("p (r c) -> p r c", c=SW))
                        dve.tensor_tensor(o, src[:, 8 * q + t:8 * q + t + 7, :], wt, ALU.mult)
                    dve.drain()
                    if t:
                        o = rows_s[:, :, 1:1 + SW]
                        dve.tensor_tensor(o, o, prod_s[:].rearrange("p (r c) -> p r c", c=SW), ALU.add)
                        dve.drain()
                pv = prod_s[:, 0:PIX].rearrange("p (r c) -> p r c", c=W)
                for t in range(4):
                    for q in range(8):
                        wt = wres[:, t * H + 7 * q:t * H + 7 * q + 7].unsqueeze(1).to_broadcast([128, H, 7])
                        o = (up_s[s][:] if t == 0 else pv)[:, :, 7 * q:7 * q + 7]
                        dve.tensor_tensor(o, rows_s[:, :, 8 * q + t:8 * q + t + 7], wt, ALU.mult)
                    dve.drain()
                    if t:
                        dve.tensor_tensor(up_s[s][:], up_s[s][:], pv, ALU.add)
                        dve.drain()

            fp = fpad[:, 0:TS_ * TS_].rearrange("p (r c) -> p r c", c=TS_)[:, 1:1 + H, 1:1 + W]
            wbat = const("wbat")

            def table_image(i, first):
                if not first:
                    dve.wait_ge(s_tmm, i * NBLK)
                dve.tensor_copy(bcol[:], wbat[:, bass.ds(i * 2, 2)])
                dve.drain()
                dve.tensor_scalar(fp, up_s[0][:], bcol[:, 0:1], None, ALU.mult)
                dve.drain()
                dve.scalar_tensor_tensor(out=fp, in0=up_s[1][:], scalar=bcol[:, 1:2], in1=fp,
                                         op0=ALU.mult, op1=ALU.add)
                dve.drain()
                if not first:
                    dve.wait_ge(s_fst, i * 16)
                dve.tensor_scalar(fdense[:].rearrange("p (r c) -> p r c", c=W), fp, 2.0, None,
                                  ALU.mult).then_inc(s_up, 1)
                for r in range(1, NBLK, 2):
                    s = r % NTB
                    if not (first and r < NTB):
                        dve.wait_ge(s_tst[s], i * (16 * TB_USES[s]) + 16 * (r // NTB))
                    dve.wait_ge(s_tmm, i * NBLK + r + 1)
                    dve.tensor_copy(tst[s][:], bank[s][:, :].rearrange("p (q g c) -> p g q c", q=4, g=G)
                                    ).then_inc(s_tev[s], 1)

            table_image(0, True)
            with dve.Fori(1, NIMG) as i:
                table_image(i, False)

            dve.wait_ge(s_fst, 16 * NIMG)
            for s in range(NTB):
                dve.wait_ge(s_tst[s], 16 * NIMG * TB_USES[s])
            dve.wait_ge(s_w, 16 * 14)
            dve.memset(xpad[:], 0.0)
            dve.memset(qbd[:], 0.0)
            dve.memset(ofp[:], 0.0)
            dve.memset(xd[:], 0.0)
            dve.memset(fx[:], 0.0)
            dve.memset(hxt[:], 0.0)
            for s in range(2):
                dve.memset(osb[s][:], 0.0)
            dve.tensor_tensor(kyxb[:], bom[:, 0:2 * S], const("kyx"), ALU.add).then_inc(s_mz, 1)

            def x_pos(i):
                xv = xw[:].rearrange("p (h w) -> p h w", w=W)
                for k in range(9):
                    dve.drain()
                    if k == 0:
                        dve.wait_ge(s_xc, i + 1)
                    y, x = k // 3, k % 3
                    last = dve.scalar_tensor_tensor(out=xv, in0=xpad[:, 1 + y:1 + y + H, 1 + x:1 + x + W],
                                                    scalar=posw[:, k:k + 1], in1=xv, op0=ALU.mult, op1=ALU.add)
                last.then_inc(s_xpos, 1)

            def x_qkv(i, bands):
                if bands[0] == 0:
                    x_pos(i)
                def centre(b):
                    dve.wait_ge(s_mean, i * NB + b + 1)
                    dve.tensor_tensor(ln_bufs(b)[0], band(xw, b), bank[0][:, 0:BAND], ALU.subtract).then_inc(s_d, 1)

                def norm(b):
                    d, r = ln_bufs(b)
                    dve.wait_ge(s_sd, i * NB + b + 1)
                    dve.reciprocal(r, r)
                    dve.drain()
                    dve.tensor_tensor(d, d, r, ALU.mult)

                centre(bands[0])
                centre(bands[1])
                norm(bands[0])
                for b in bands:
                    n = i * NB + b + 1
                    mm = i * (5 * NB) + 5 * b
                    d = ln_bufs(b)[0]
                    dve.drain()
                    dve.tensor_scalar(win(yw[:]), img(b)(d), col(G1), col(B1), ALU.mult, ALU.add).then_inc(s_y, 1)
                    if b < bands[-1]:
                        norm(b + 1)
                    if b + 2 in bands:
                        centre(b + 2)
                    for m in range(2):
                        j0, j1 = 4 * m, min(4 * m + 4, NWIN)
                        if m == 0 and not (isinstance(i, int) and i == 0 and b == 0):
                            dve.wait_ge(s_vst, i * (16 * NB) + 16 * b)
                        dve.wait_ge(s_mm, mm + 4 + m)
                        last = dve.tensor_tensor(
                            vb[:, j0:j1, :], bank[5 + m][0:64, 0:(j1 - j0) * C].rearrange("p (w c) -> p w c", c=C),
                            bvrow[:].unsqueeze(1).to_broadcast([64, j1 - j0, C]), ALU.add)
                    last.then_inc(s_v, 1)
                    if b == bands[-1]:
                        dve.wait_ge(s_vc, n)
                    dve.wait_ge(s_k, n)
                    dve.tensor_reduce(qm[:, b * NWIN:(b + 1) * NWIN], qb[b % 2][:].rearrange("p (w n) -> p w n", n=W2),
                                      AX.X, ALU.add)
                    dve.tensor_reduce(km[:, b * NWIN:(b + 1) * NWIN], kb[b % 2][:].rearrange("p (w n) -> p w n", n=W2),
                                      AX.X, ALU.add).then_inc(s_qm, 1)

            def x_route(i):
                dve.wait_ge(s_lg, i + 1)
                dve.tensor_scalar(lg[0:P2, :], bank[7][0:P2, 0:P2], 1.0 / (W2 * W2), None, ALU.mult)
                dve.drain()
                dve.max(mx8[0:P2, :], lg[0:P2, :])
                dve.drain()
                dve.max_index(ix8[0:P2, :], mx8[0:P2, :], lg[0:P2, :]).then_inc(s_ix, 1)

            def x_band(i, b, pending):
                base = i * P2 + b * NWIN
                olv = ol[:].rearrange("p (r c) -> p r c", c=W)

                def lepe(b, k):
                    y, x = k // 5, k % 5
                    v = xpad[:, b * WS + y:b * WS + y + WS, x:x + W]
                    if k == 0:
                        dve.tensor_scalar(olv, v, lepw[:, 0:1], col(LB), ALU.mult, ALU.add)
                    else:
                        dve.drain()
                        dve.scalar_tensor_tensor(out=olv, in0=v, scalar=lepw[:, k:k + 1], in1=olv,
                                                 op0=ALU.mult, op1=ALU.add)

                def maxes(j):
                    n = b * NWIN + j
                    dve.wait_ge(s_sc, base + j + 1)
                    dve.tensor_reduce(nmx[n % 2][:], bank[2 + n % 2][:].rearrange("p (h k) -> p h k", h=2),
                                      AX.X, ALU.max, negate=True).then_inc(s_mx, 1)

                def scale_heads(j):
                    n = b * NWIN + j
                    dve.wait_ge(s_ex, base + j + 1)
                    dve.reciprocal(rinv[n % 2][:], sm[n % 3][:])
                    dve.drain()
                    dve.wait_ge(s_pv, base + j + 1)
                    for g in range(2):
                        q = slice(64 * g, 64 * g + 64)
                        o, x = (v[q, 0:C].rearrange("p (h g d) -> p h g d", h=2, g=2)[:, :, g, :]
                                for v in (osb[n % 2], bank[6]))
                        last = dve.tensor_tensor(o, x, rinv[n % 2][q, :].unsqueeze(2).to_broadcast([64, 2, HD]), ALU.mult)
                    last.then_inc(s_os, 1)

                left = list(range(EARLY[0] + EARLY[1] if b else 0, 25))
                step = -(-len(left) // (NWIN + 2))
                for t in range(NWIN + 2):
                    if t < NWIN:
                        maxes(t)
                    if t == 0 and b == 0:
                        dve.wait_ge(s_vc, i * NB + NB)
                    for k in left[step * t:step * (t + 1)]:
                        lepe(b, k)
                    if 0 <= t - 2 < NWIN:
                        scale_heads(t - 2)
                dve.drain()
                dve.wait_ge(s_ot, i * NB + b + 1)
                olr = img(b)(ol[:])
                dve.tensor_tensor(olr, olr, win(bank[7][:, 0:BAND]), ALU.add).then_inc(s_ol, 1)
                n = i * NB + b + 1
                post = i * (7 * NB) + 7 * b
                dve.wait_ge(s_post, post + 1)
                dve.scalar_tensor_tensor(out=band(xw, b), in0=bank[0][:, 0:BAND], scalar=col(BO), in1=band(xw, b),
                                         op0=ALU.add, op1=ALU.add).then_inc(s_xa, 1)
                dve.drain()
                dve.wait_ge(s_post, post + 2)
                dve.tensor_tensor(t1[:], band(xw, b), bank[1][:, 0:BAND], ALU.subtract).then_inc(s_d2, 1)
                if b + 1 < NB:
                    for k in range(EARLY[0]):
                        lepe(b + 1, k)
                dve.wait_ge(s_sd2, n)
                dve.reciprocal(t2[:], t2[:])
                dve.drain()
                dve.tensor_tensor(t1[:], t1[:], t2[:], ALU.mult)
                dve.drain()
                dve.tensor_scalar(yw[:], t1[:], col(G2), col(B2), ALU.mult, ALU.add).then_inc(s_z2, 1)
                if b + 1 < NB:
                    for k in range(EARLY[0], EARLY[0] + EARLY[1]):
                        lepe(b + 1, k)
                if pending is not None:
                    weigh_gathered(pending, min(NSLOT * (b + 2), NT - NSLOT))
                dve.wait_ge(s_post, post + 7)
                dve.scalar_tensor_tensor(out=band(xw, b), in0=bank[5][:, 0:BAND], scalar=col(M2), in1=band(xw, b),
                                         op0=ALU.add, op1=ALU.add).then_inc(s_xm, 1)

            def x_offsets(i, pending):
                dve.drain()
                dve.tensor_reduce(pool1[:, 3:4], xw[:], AX.X, ALU.add)
                dve.drain()
                dve.tensor_scalar(pool1[:, 0:1], pool1[:, 3:4], 1.0 / PIX, None, ALU.mult).then_inc(s_pl, 1)
                dve.wait_ge(s_ge, i + 1)
                dve.tensor_scalar(pool1[:, 2:3], pool1[:, 2:3], 1.0, None, ALU.add)
                dve.drain()
                dve.reciprocal(pool1[:, 3:4], pool1[:, 2:3])
                dve.drain()
                dve.tensor_scalar(pool1[:, 3:4], pool1[:, 3:4], 1.0, None, ALU.add)
                dve.drain()
                for b in range(NB):
                    if b >= 2:
                        dve.wait_ge(s_p5, i * NB + b - 1)
                    dve.tensor_scalar((t1, t2)[b % 2][:], band(xw, b), pool1[:, 3:4], None, ALU.mult).then_inc(s_fi, 1)
                    if b in (1, 3) and pending is not None:
                        weigh_gathered(pending, NT - 2 + b // 2)

            def positions(i, t):
                dve.wait_ge(s_om, i * NT + t + 1)
                dve.tensor_tensor(msk[:], bank[0][:, 2 * S:3 * S], bom[:, 2 * S:3 * S], ALU.add).then_inc(s_mb, 1)
                dve.tensor_tensor(tmp[:], bank[0][:, 0:2 * S], kyxb[:], ALU.add)
                dve.drain()
                dve.tensor_scalar(pyx[:, 0:S], tmp[:, 0:S], const("posy")[:, t:t + 1], -1.0, ALU.add, ALU.max)
                dve.tensor_scalar(pyx[:, S:], tmp[:, S:], const("posx")[:, t:t + 1], -1.0, ALU.add, ALU.max)
                dve.drain()
                dve.tensor_scalar(pyx[:], pyx[:], float(H), None, ALU.min)
                dve.drain()
                dve.tensor_tensor(hxt[:, :, 0:W], pyx[:, S + NS:].unsqueeze(2).to_broadcast([128, NH, W]),
                                  const("iota")[:, 0:W].unsqueeze(1).to_broadcast([128, NH, W]), ALU.subtract).then_inc(s_hx, 1)
                dve.tensor_scalar(pyr[:], pyx[:, NS:S], -float(t * 128 // SP57), None, ALU.add)
                dve.drain()
                dve.tensor_tensor(wy[:], pyr[:].unsqueeze(2).to_broadcast([128, NH, WR]),
                                  const("rowk").rearrange("p (h r) -> p h r", r=WR), ALU.subtract)
                dve.drain()
                reach = (window_rows(t) - 1) / 2
                dve.tensor_scalar(vio[:], wy[:, :, 0], -reach, None, ALU.add).then_inc(s_wy, 1)
                dve.drain()
                dve.tensor_reduce(vmx[:, 0:1], vio[:], AX.X, ALU.max, apply_absolute_value=True)
                dve.drain()
                dve.tensor_scalar(vmx[:, 1:2], vmx[:, 0:1], reach, None, ALU.is_gt).then_inc(s_vm, 1)

            def indices(i, t):
                s = t % NSLOT
                dve.tensor_scalar(fl[:], pyx[:], MAGIC, None, ALU.add)
                dve.wait_ge(s_me, i * NT + t + 1)
                dve.tensor_scalar(msk[:], msk[:], 1.0, None, ALU.add)
                dve.drain()
                dve.tensor_scalar(fl[:], fl[:], -MAGIC, None, ALU.add)
                dve.reciprocal(msk[:], msk[:])
                dve.drain()
                dve.tensor_tensor(tmp[:], fl[:], pyx[:], ALU.is_gt)
                dve.drain()
                dve.tensor_tensor(fl[:], fl[:], tmp[:], ALU.subtract)
                dve.drain()
                dve.scalar_tensor_tensor(out=tmp[:, 0:S], in0=fl[:, 0:S], scalar=float(TS_), in1=fl[:, S:],
                                         op0=ALU.mult, op1=ALU.add)
                dve.tensor_tensor(pyx[:], pyx[:], fl[:], ALU.subtract)
                dve.drain()
                dve.scalar_tensor_tensor(out=idx[s][:], in0=tmp[:, 0:S], scalar=float(G), in1=gimg[:],
                                         op0=ALU.mult, op1=ALU.add).then_inc(s_ir, 1)
                dve.tensor_tensor(ady[:, :, 1], pyx[:, 0:S], msk[:], ALU.mult)
                dve.wait_ge(s_wy2, i * NT + t + 1)
                dve.tensor_tensor(wy[:], wy[:], msk[:, NS:].unsqueeze(2).to_broadcast([128, NH, WR]), ALU.mult)
                dve.drain()
                dve.tensor_tensor(ady[:, :, 0], msk[:], ady[:, :, 1], ALU.subtract)
                dve.drain()
                dve.tensor_tensor(wts[s][:, :, :, 1], ady[:], pyx[:, S:].unsqueeze(2).to_broadcast([128, S, 2]), ALU.mult)
                dve.drain()
                dve.tensor_tensor(wts[s][:, :, :, 0], ady[:], wts[s][:, :, :, 1], ALU.subtract)
                dve.wait_ge(s_fm, i * NT + t + 1)
                if not (isinstance(i, int) and i == 0):
                    dve.wait_ge(s_fbd, i * NT + t + 1 - NT)
                dve.tensor_scalar(flag[0:1, t:t + 1], bank[0][0:1, 0:1], 0.0, None, ALU.is_gt).then_inc(s_fl, 1)
                dve.drain()

            def weigh_windows(i, t):
                v = vh[t % NVH][:].rearrange("p (q j a c) -> p q a j c", q=4, j=4, a=2)
                wr = window_rows(t)
                w = wy[:, :, 0:wr].rearrange("p (q j a) r -> p q a j r", q=4, j=4)

                def add_up(n):
                    dve.tensor_reduce(v[:, n // 2, n % 2], prod[:, n % 2, :, 0:wr].rearrange("p j r c -> p j c r"),
                                      AX.X, ALU.add)

                for n in range(8):
                    q, a = n // 2, n % 2
                    dve.wait_ge(s_hm, i * (8 * NT) + 8 * t + n + 1)
                    dve.tensor_tensor(
                        prod[:, a, :, 0:wr], bank[1 + 2 * (q % 2) + a][:].rearrange("p (j r c) -> p j r c", j=4, r=WR)[:, :, 0:wr],
                        w[:, q, a].unsqueeze(3).to_broadcast([128, 4, wr, CG]), ALU.mult).then_inc(s_hp, 1)
                    if n:
                        add_up(n - 1)
                    dve.drain()
                add_up(7)
                dve.drain()

            def weigh_gathered(i, t):
                s = t % NSLOT
                n = i * NT + t + 1
                g = gbuf[s][:].rearrange("p s y x c -> p (s y x) c")
                w = wts[s][:].rearrange("p s y x -> p (s y x)")
                dve.drain()
                dve.wait_ge(s_gs, n)
                dve.sem_inc(s_hold["dve"], 1)
                dve.wait_ge(s_g[s], 16 * NS)
                dve.tensor_tensor(g, g, w[:, 0:4 * NS].unsqueeze(2).to_broadcast([128, 4 * NS, CG]), ALU.mult)
                dve.drain()
                dy = [gbuf[s][:, :, y].rearrange("p s x c -> p s (x c)") for y in range(2)]
                dve.tensor_tensor(dy[0], dy[0], dy[1], ALU.add)
                dve.drain()

            def samples(i, t):
                s = t % NSLOT
                if t == NT - 1:
                    dve.tensor_tensor(lastval.rearrange("p (s c) -> p s c", c=CG), gbuf[s][:, :, 0, 0, :],
                                      gbuf[s][:, :, 0, 1, :], ALU.add).then_inc(s_lval, 1)
                    return
                if t:
                    dve.wait_ge(s_vt, i * (3 * NT) + 3 * t)
                elif not (isinstance(i, int) and i == 0):
                    dve.wait_ge(s_vt, i * (3 * NT))
                dve.tensor_tensor(val[:].rearrange("p (s c) -> p s c", c=CG), gbuf[s][:, :, 0, 0, :],
                                  gbuf[s][:, :, 0, 1, :], ALU.add).then_inc(s_val, 1)

            def general(i, t):
                s = t % NSLOT
                w = wts[s][:].rearrange("p s y x -> p (s y x)")
                f = dve.value_load(flag[0:1, t:t + 1], min_val=0, max_val=1)
                with dve.If(f > 0):
                    dve.drain()
                    dve.wait_ge(s_fbd, i * NT + t + 1)
                    dve.sem_inc(s_hold["dve"], 1)
                    p3 = hxt[:].rearrange("p h (q c) -> p (h q) c", c=CG)
                    dve.tensor_tensor(p3, p3, w[:, 4 * NS:].unsqueeze(2).to_broadcast([128, 4 * NH, CG]), ALU.mult)
                    dve.drain()
                    dve.tensor_tensor(hxt[:, :, 0:2 * CG], hxt[:, :, 0:2 * CG], hxt[:, :, 2 * CG:], ALU.add)
                    dve.drain()
                    dve.tensor_tensor(vh[t % NVH][:].rearrange("p (h c) -> p h c", c=CG), hxt[:, :, 0:CG],
                                      hxt[:, :, CG:2 * CG], ALU.add)
                dve.drain().then_inc(s_vh, 1)

            def finish(i, t):
                dve.wait_ge(s_rt, i * NT + t + 1)
                x = xd[:, t * 128:(t + 1) * 128]
                dve.tensor_tensor(x, x, rt[:], ALU.add).then_inc(s_fin, 1)

            def d_block(i, k, tail, weighed):
                if k == 0 and tail:
                    for t in range(NT - NSLOT, NT):
                        general(i - 1, t)
                    samples(i - 1, NT - 1)
                if k == 0:
                    dve.tensor_scalar(gimg[:], const("gidx"), const("ibase")[:, bass.ds(i, 1)], None, ALU.add)
                    dve.drain()
                for t in range(NSLOT * k, min(NSLOT * (k + 1), NT)):
                    if t >= NSLOT:
                        general(i, t - NSLOT)
                    positions(i, t)
                    if t >= NSLOT:
                        if not (weighed and t == NSLOT * k):
                            weigh_gathered(i, t - NSLOT)
                        samples(i, t - NSLOT)
                    elif t == 0 and tail:
                        samples(i - 1, NT - 3)
                    indices(i, t)
                    if t >= NVH:
                        finish(i, t - NVH)
                    elif t == 0 and tail:
                        finish(i - 1, NT - 4)
                        samples(i - 1, NT - 2)
                        for u in range(NT - 3, NT):
                            finish(i - 1, u)
                    weigh_windows(i, t)

            def body(xi, di, tail):
                for k in range(9):
                    if di is not None:
                        d_block(di, k, tail, xi is not None and k > 2)
                    if xi is None:
                        continue
                    if k == 0:
                        x_qkv(xi, range(0, 3))
                    elif k == 1:
                        x_qkv(xi, range(3, NB))
                        x_route(xi)
                    else:
                        x_band(xi, k - 2, di)
                    if k == 8:
                        x_offsets(xi, di)

            body(0, None, False)
            body(1, 0, False)
            with dve.Fori(2, NIMG) as i:
                body(i, i - 1, True)
            body(None, NIMG - 1, True)
            for t in range(NT - NSLOT, NT):
                general(NIMG - 1, t)
                weigh_gathered(NIMG - 1, t)
                samples(NIMG - 1, t)
                finish(NIMG - 1, t - 1)
            finish(NIMG - 1, NT - 1)


def kernel(**inputs):
    import concourse.bacc as bacc
    from concourse.bass_utils import run_bass_kernel_spmd

    v = {k: np.asarray(x) for k, x in inputs.items()}
    om = v["L1_conv_w_offmask"].reshape(3 * S, C, KK)
    order = np.array([(g * KK + k) * 2 + d for d in range(2) for g, k in ORDER] + [2 * S + g * KK + k for g, k in ORDER])
    qkv_b = v["L0_conv_qkv_b"]
    m1 = v["L0_conv_mlp_b1"]
    dcn = v["L1_conv_w_dcn"].reshape(C, C, KK).transpose(1, 2, 0)
    arrays = {
        "x": v["x"].reshape(B, C, PIX),
        "feat_s": v["L1_conv_feat_s"].reshape(2, C, SH * SW),
        "consts": constants(),
        "qkv_w": v["L0_conv_qkv_w"], "wo_w": v["L0_conv_wo_w"],
        "mlp_w1": v["L0_conv_mlp_w1"], "mlp_w2": v["L0_conv_mlp_w2"],
        "w_fsm_t": v["L1_conv_w_fsm"].T, "w_atten_t": v["L1_conv_w_atten"].T, "w_off_t": v["L1_conv_w_off"].T,
        "w_om_t": om[order].transpose(1, 2, 0),
        "w_dcn_t": np.stack([dcn[g * CG:(g + 1) * CG, k] for g, k in ORDER]).reshape(KK, 128, C).transpose(1, 0, 2),
        "pos_w": v["L0_conv_pos_w"].reshape(C, 9), "lepe_w": v["L0_conv_lepe_w"].reshape(C, 25),
        "cols": np.stack([v["L0_conv_pos_b"], v["L0_conv_ln1_g"], v["L0_conv_ln1_b"], qkv_b[0:C], qkv_b[C:2 * C],
                          qkv_b[2 * C:], v["L0_conv_lepe_b"], v["L0_conv_wo_b"], v["L0_conv_ln2_g"],
                          v["L0_conv_ln2_b"], v["L0_conv_mlp_b2"], v["L1_conv_b_dcn"],
                          m1[0:C], m1[C:2 * C], m1[2 * C:]], axis=1),
        "bv": qkv_b[2 * C:],
        "b_om": v["L1_conv_b_offmask"][order],
    }
    arrays = {k: np.ascontiguousarray(x) for k, x in arrays.items()}
    nc = bacc.Bacc("TRN2", target_bir_lowering=False, num_devices=1)
    aps = {k: nc.dram_tensor("in_" + k, x.shape, mybir.dt.from_np(x.dtype), kind="ExternalInput").ap()
           for k, x in arrays.items()}
    out = nc.dram_tensor("out", (B, C, H, W), F32, kind="ExternalOutput").ap()
    build(nc, aps, out)
    r = run_bass_kernel_spmd(nc, [{"in_" + k: x for k, x in arrays.items()}], core_ids=[0])
    return r.results[0]["out"]
```
